# Optimizing a Trainium2 kernel written in Bass

```python
import numpy as np
import jax
import jax.numpy as jnp

def _softmax(x, axis=-1):
    return jax.nn.softmax(x, axis=axis)

def _gelu(x):
    return jax.nn.gelu(x, approximate=True)

def _silu(x):
    return jax.nn.silu(x)

def _sigmoid(x):
    return jax.nn.sigmoid(x)

def _layernorm(x, axis=-1, eps=1e-05):
    m = jnp.mean(x, axis=axis, keepdims=True)
    v = jnp.var(x, axis=axis, keepdims=True)
    return (x - m) / jnp.sqrt(v + eps)

def _scatter_add(tgt, idx, src, axis=0):
    return tgt.at[idx].add(src)

def _segment_sum(src, seg, n):
    return jax.ops.segment_sum(src, seg, n)
kernel_name = 'mk_perceiver_d1_seqx_r4_0f7a23'

def setup_inputs(seed: int=0):
    np.random.seed(seed)
    _w = jnp.asarray

    def _rec_inputs():
        import jax
        import jax.numpy as jnp
        _rk = jax.random.key(seed)
        x = -0.0002928 + 1 * jax.random.normal(jax.random.fold_in(_rk, 1), (8, 64, 256), jnp.float32)
        _lenS = 64 - jax.random.randint(jax.random.fold_in(_rk, 7), (8,), 0, max(1, 64 // 4) + 1, jnp.int32)
        _lenS2 = 1601 - jax.random.randint(jax.random.fold_in(_rk, 8), (8,), 0, max(1, 1601 // 4) + 1, jnp.int32)
        _ctx_1024P = jax.random.normal(jax.random.fold_in(_rk, 11), (8, 16, 256), jnp.float32)
        _ctx_1024c = jax.random.dirichlet(jax.random.fold_in(_rk, 511), 0.3 * jnp.ones((16,), jnp.float32), (8, 1601))
        _ctx_1024t = jnp.einsum('bsk,bkd->bsd', _ctx_1024c, _ctx_1024P)
        _ctx_1024t = _ctx_1024t * jax.lax.rsqrt(jnp.mean(jnp.square(_ctx_1024t)) + 1e-12) * 0.953939
        ctx_1024 = 4.13588e-05 + 0.999923 * (_ctx_1024t + 0.3 * jax.random.normal(jax.random.fold_in(_rk, 611), (8, 1601, 256), jnp.float32))
        _validS = jnp.arange(64)[None, :] < _lenS[:, None]
        _validS2 = jnp.arange(1601)[None, :] < _lenS2[:, None]
        _causal = jnp.tril(jnp.ones((64, 64), dtype=bool))
        mask_BxSxS2_bf0 = jnp.logical_not(jnp.ones((8, 64, 1601), dtype=bool))
        return (x, ctx_1024, mask_BxSxS2_bf0)
    x, ctx_1024, mask_BxSxS2_bf0 = _rec_inputs()

    def _L0_xattn_setup():
        import jax, jax.numpy as jnp
        import numpy as np
        HIDDEN = 256
        HEADS = 16
        D_K = HIDDEN // HEADS
        B, LQ, LKV = (4, 256, 512)
        NEG_INF = -1e+18
        key = jax.random.key(seed)
        ks = jax.random.split(key, 12)
        s = 1.0 / np.sqrt(HIDDEN)
        return {'tgt': jax.random.normal(ks[0], (B, LQ, HIDDEN), jnp.float32), 'memory': jax.random.normal(ks[1], (B, LKV, HIDDEN), jnp.float32), 'mask': jnp.zeros((B, LQ, LKV), dtype=bool), 'Wq': jax.random.normal(ks[2], (HIDDEN, HIDDEN), jnp.float32) * s, 'bq': jnp.zeros((HIDDEN,), jnp.float32), 'Wk': jax.random.normal(ks[3], (HIDDEN, HIDDEN), jnp.float32) * s, 'bk': jnp.zeros((HIDDEN,), jnp.float32), 'Wv': jax.random.normal(ks[4], (HIDDEN, HIDDEN), jnp.float32) * s, 'bv': jnp.zeros((HIDDEN,), jnp.float32), 'Wo': jax.random.normal(ks[5], (HIDDEN, HIDDEN), jnp.float32) * s, 'bo': jnp.zeros((HIDDEN,), jnp.float32)}
    _L0_xattn_all = _L0_xattn_setup()
    _L0_xattn_in = {k: v for k, v in _L0_xattn_all.items() if k in ('Wq', 'bq', 'Wk', 'bk', 'Wv', 'bv', 'Wo', 'bo')}
    del _L0_xattn_all

    def _L0_attn_setup():
        import jax, jax.numpy as jnp
        import numpy as np
        E = 256
        H = 16
        D = E // H

        def _mha(x, Wq, bq, Wk, bk, Wv, bv, Wo, bo):
            q = jnp.einsum('bse,hde->bhsd', x, Wq) + bq[None, :, None, :]
            k = jnp.einsum('bse,hde->bhsd', x, Wk) + bk[None, :, None, :]
            v = jnp.einsum('bse,hde->bhsd', x, Wv) + bv[None, :, None, :]
            scores = jnp.einsum('bhsd,bhtd->bhst', q, k) / jnp.sqrt(jnp.asarray(D, x.dtype))
            w = jax.nn.softmax(scores, axis=-1)
            o = jnp.einsum('bhst,bhtd->bhsd', w, v)
            B, _, S, _ = o.shape
            o = jnp.transpose(o, (0, 2, 1, 3)).reshape(B, S, H * D)
            return o @ Wo.T + bo
        key = jax.random.key(seed)
        ks = jax.random.split(key, 9)
        s = 0.02
        return {'hidden_state': jax.random.normal(ks[0], (4, 256, E), jnp.float32), 'Wq': jax.random.normal(ks[1], (H, D, E), jnp.float32) * s, 'bq': jax.random.normal(ks[2], (H, D), jnp.float32) * s, 'Wk': jax.random.normal(ks[3], (H, D, E), jnp.float32) * s, 'bk': jax.random.normal(ks[4], (H, D), jnp.float32) * s, 'Wv': jax.random.normal(ks[5], (H, D, E), jnp.float32) * s, 'bv': jax.random.normal(ks[6], (H, D), jnp.float32) * s, 'Wo': jax.random.normal(ks[7], (E, E), jnp.float32) * s, 'bo': jax.random.normal(ks[8], (E,), jnp.float32) * s}
    _L0_attn_all = _L0_attn_setup()
    _L0_attn_in = {k: v for k, v in _L0_attn_all.items() if k in ('Wq', 'bq', 'Wk', 'bk', 'Wv', 'bv', 'Wo', 'bo')}
    del _L0_attn_all

    def _L0_ffn_setup():
        import jax, jax.numpy as jnp
        import numpy as np
        DIM = 256

        def _reference_tuple_inner(x, W_r, W_k, W_v, mu_r, mu_k):
            B, T, C = x.shape
            x_prev = jnp.concatenate([jnp.zeros((B, 1, C), x.dtype), x[:, :-1, :]], axis=1)
            xr = mu_r * x + (1.0 - mu_r) * x_prev
            xk = mu_k * x + (1.0 - mu_k) * x_prev
            r = jax.nn.sigmoid(jnp.einsum('btc,dc->btd', xr, W_r))
            k = jnp.einsum('btc,dc->btd', xk, W_k)
            k_act = jnp.square(jax.nn.relu(k))
            out = r * jnp.einsum('btc,dc->btd', k_act, W_v)
            new_state = x[:, -1, :]
            return (out, new_state)
        key = jax.random.key(seed)
        ks = jax.random.split(key, 6)
        B, T, C = (8, 512, DIM)
        x = jax.random.normal(ks[0], (B, T, C), dtype=jnp.float32)
        s = 1.0 / np.sqrt(C)
        W_r = jax.random.uniform(ks[1], (C, C), jnp.float32, -s, s)
        W_k = jax.random.uniform(ks[2], (C, C), jnp.float32, -s, s)
        W_v = jax.random.uniform(ks[3], (C, C), jnp.float32, -s, s)
        mu_r = jax.random.uniform(ks[4], (C,), jnp.float32)
        mu_k = jax.random.uniform(ks[5], (C,), jnp.float32)
        return {'x': x, 'W_r': W_r, 'W_k': W_k, 'W_v': W_v, 'mu_r': mu_r, 'mu_k': mu_k}
    _L0_ffn_all = _L0_ffn_setup()
    _L0_ffn_in = {k: v for k, v in _L0_ffn_all.items() if k in ('W_r', 'W_k', 'W_v', 'mu_r', 'mu_k')}
    del _L0_ffn_all
    return {'x': x, 'ctx_1024': ctx_1024, 'mask_BxSxS2_bf0': mask_BxSxS2_bf0, 'L0_xattn_Wq': _L0_xattn_in['Wq'], 'L0_xattn_bq': _L0_xattn_in['bq'], 'L0_xattn_Wk': _L0_xattn_in['Wk'], 'L0_xattn_bk': _L0_xattn_in['bk'], 'L0_xattn_Wv': _L0_xattn_in['Wv'], 'L0_xattn_bv': _L0_xattn_in['bv'], 'L0_xattn_Wo': _L0_xattn_in['Wo'], 'L0_xattn_bo': _L0_xattn_in['bo'], 'L0_attn_Wq': _L0_attn_in['Wq'], 'L0_attn_bq': _L0_attn_in['bq'], 'L0_attn_Wk': _L0_attn_in['Wk'], 'L0_attn_bk': _L0_attn_in['bk'], 'L0_attn_Wv': _L0_attn_in['Wv'], 'L0_attn_bv': _L0_attn_in['bv'], 'L0_attn_Wo': _L0_attn_in['Wo'], 'L0_attn_bo': _L0_attn_in['bo'], 'L0_ffn_W_r': _L0_ffn_in['W_r'], 'L0_ffn_W_k': _L0_ffn_in['W_k'], 'L0_ffn_W_v': _L0_ffn_in['W_v'], 'L0_ffn_mu_r': _L0_ffn_in['mu_r'], 'L0_ffn_mu_k': _L0_ffn_in['mu_k']}

def reference(x, ctx_1024, mask_BxSxS2_bf0, L0_xattn_Wq, L0_xattn_bq, L0_xattn_Wk, L0_xattn_bk, L0_xattn_Wv, L0_xattn_bv, L0_xattn_Wo, L0_xattn_bo, L0_attn_Wq, L0_attn_bq, L0_attn_Wk, L0_attn_bk, L0_attn_Wv, L0_attn_bv, L0_attn_Wo, L0_attn_bo, L0_ffn_W_r, L0_ffn_W_k, L0_ffn_W_v, L0_ffn_mu_r, L0_ffn_mu_k):
    import jax
    import jax.numpy as jnp

    def _L0_xattn_ref(tgt, memory, mask, Wq, bq, Wk, bk, Wv, bv, Wo, bo):
        import jax, jax.numpy as jnp
        import numpy as np
        HIDDEN = 256
        HEADS = 16
        D_K = HIDDEN // HEADS
        B, LQ, LKV = (4, 256, 512)
        NEG_INF = -1e+18
        b = tgt.shape[0]

        def heads(x):
            return x.reshape(b, -1, HEADS, D_K).transpose(0, 2, 1, 3)
        q = heads(tgt @ Wq + bq) / jnp.sqrt(jnp.asarray(D_K, tgt.dtype))
        k = heads(memory @ Wk + bk)
        v = heads(memory @ Wv + bv)
        scores = jnp.einsum('bhqd,bhkd->bhqk', q, k)
        scores = jnp.where(mask[:, None, :, :], NEG_INF, scores)
        attn = jax.nn.softmax(scores, axis=-1)
        ctx = jnp.einsum('bhqk,bhkd->bhqd', attn, v)
        ctx = ctx.transpose(0, 2, 1, 3).reshape(b, -1, HIDDEN)
        return ctx @ Wo + bo

    def _L0_attn_ref(hidden_state, Wq, bq, Wk, bk, Wv, bv, Wo, bo):
        import jax, jax.numpy as jnp
        import numpy as np
        E = 256
        H = 16
        D = E // H

        def _mha(x, Wq, bq, Wk, bk, Wv, bv, Wo, bo):
            q = jnp.einsum('bse,hde->bhsd', x, Wq) + bq[None, :, None, :]
            k = jnp.einsum('bse,hde->bhsd', x, Wk) + bk[None, :, None, :]
            v = jnp.einsum('bse,hde->bhsd', x, Wv) + bv[None, :, None, :]
            scores = jnp.einsum('bhsd,bhtd->bhst', q, k) / jnp.sqrt(jnp.asarray(D, x.dtype))
            w = jax.nn.softmax(scores, axis=-1)
            o = jnp.einsum('bhst,bhtd->bhsd', w, v)
            B, _, S, _ = o.shape
            o = jnp.transpose(o, (0, 2, 1, 3)).reshape(B, S, H * D)
            return o @ Wo.T + bo
        return _mha(hidden_state, Wq, bq, Wk, bk, Wv, bv, Wo, bo)

    def _L0_ffn_ref(x, W_r, W_k, W_v, mu_r, mu_k):
        import jax, jax.numpy as jnp
        import numpy as np
        DIM = 256

        def _reference_tuple_inner(x, W_r, W_k, W_v, mu_r, mu_k):
            B, T, C = x.shape
            x_prev = jnp.concatenate([jnp.zeros((B, 1, C), x.dtype), x[:, :-1, :]], axis=1)
            xr = mu_r * x + (1.0 - mu_r) * x_prev
            xk = mu_k * x + (1.0 - mu_k) * x_prev
            r = jax.nn.sigmoid(jnp.einsum('btc,dc->btd', xr, W_r))
            k = jnp.einsum('btc,dc->btd', xk, W_k)
            k_act = jnp.square(jax.nn.relu(k))
            out = r * jnp.einsum('btc,dc->btd', k_act, W_v)
            new_state = x[:, -1, :]
            return (out, new_state)
        return _reference_tuple_inner(x, W_r, W_k, W_v, mu_r, mu_k)[0]
    x = x + _L0_xattn_ref(_layernorm(x, axis=-1), ctx_1024, mask_BxSxS2_bf0, L0_xattn_Wq, L0_xattn_bq, L0_xattn_Wk, L0_xattn_bk, L0_xattn_Wv, L0_xattn_bv, L0_xattn_Wo, L0_xattn_bo)
    x = x + _L0_attn_ref(_layernorm(x, axis=-1), L0_attn_Wq, L0_attn_bq, L0_attn_Wk, L0_attn_bk, L0_attn_Wv, L0_attn_bv, L0_attn_Wo, L0_attn_bo)
    x = x + _L0_ffn_ref(_layernorm(x, axis=-1), L0_ffn_W_r, L0_ffn_W_k, L0_ffn_W_v, L0_ffn_mu_r, L0_ffn_mu_k)
    return x

_drawn_inputs = setup_inputs


def setup_inputs(seed=0):
    import zlib

    import numpy as np

    out = dict(_drawn_inputs(seed))
    spreads = {'L0_xattn_bq': (0.0, 0.402),
     'L0_xattn_bk': (0.0, 2.0),
     'L0_xattn_bv': (0.0, 0.1),
     'L0_xattn_bo': (0.0, 0.1)}
    factors = {'L0_attn_Wq': 8.0,
     'L0_attn_bq': 54.113,
     'L0_attn_Wk': 8.0,
     'L0_attn_bk': 64.0,
     'L0_attn_bv': 8.0,
     'L0_attn_bo': 3.35,
     'L0_ffn_W_r': 3.231,
     'L0_ffn_mu_r': 7.728}
    for name, (base, spread) in spreads.items():
        noise = np.random.default_rng([zlib.crc32(name.encode()), seed]).standard_normal(out[name].shape)
        drawn = base * np.exp(spread * noise) if base else spread * noise
        out[name] = jnp.asarray(drawn.astype(out[name].dtype))
    for name, factor in factors.items():
        out[name] = (out[name] * factor).astype(out[name].dtype)
    return out
```

```python
import concourse.bass as bass
from concourse import mybir
from contextlib import ExitStack

F32 = mybir.dt.float32
F32R = mybir.dt.float32r
BF16 = mybir.dt.bfloat16
U8 = mybir.dt.uint8
ALU = mybir.AluOpType
ACT = mybir.ActivationFunctionType
AX = mybir.AxisListType

P = 128

C_ID, C_PAIR, C_HEAD, C_SIDE = 0, 128, 160, 168
CONSTS = 176


class Ring:

    def __init__(self, banks, filled, freed, per_batch=0):
        self.banks, self.filled, self.freed = banks, filled, freed
        self.n, self.turns = len(banks), per_batch // len(banks)

    def bank(self, u):
        return self.banks[u % self.n]

    def count(self, u, batch):
        return batch * self.turns + u // self.n if self.turns else u // self.n

    def wait_free(self, eng, u, batch=0):
        if u >= self.n:
            eng.wait_ge(self.freed[u % self.n], self.count(u, batch))

    def wait_filled(self, eng, u, batch=0):
        eng.wait_ge(self.filled[u % self.n], self.count(u, batch) + 1)

    def last_fills(self, us):
        last = {}
        for u in us:
            last[u % self.n] = u
        return [(n, u // self.n + 1) for n, u in last.items()]

    def wait_taken(self, eng, us, batch=0):
        for n, count in self.last_fills(us):
            eng.wait_ge(self.freed[n], batch * self.turns + count if self.turns else count)


def perceiver_layer(
    nc, x, ctx, mask, Wq, bq, Wk, bk, Wv, bv, Wo, bo,
    sWq, sbq, sWk, sbk, sWv, sbv, sWo, sbo, fWr, fWk, fWv, mu_r, mu_k, consts, out,
):
    B, LQ, D = x.shape
    LK = ctx.shape[1]
    H = 16
    DK = D // H
    DH = D // P
    G = H // 2
    PAIR = 2 * DK
    KT = -(-LK // P)
    KTAIL = LK - (KT - 1) * P
    KPAD = KT * P
    CH = 402
    NCH = 4
    KS = NCH * CH
    T = B * LQ
    TJ = T // P
    LAST = B - 1
    QSCALE = -1.0 / DK ** 0.5
    MASKED = 2.0 ** 60
    PADDED = 2.0 ** 100
    EPS = 1e-5
    assert T % P == 0 and KS >= LK and CH % 2 == 0 and 2 * LQ == P

    PT_TILES = [range(0, 4), range(4, 7), range(7, 10), range(10, 13)]
    NV = NC = (KT + 1) // 2
    NK = DH * NCH
    SIDE = [
        [("V", 0), ("V", 1), ("V", 2)],
        [("V", 3), ("V", 4), ("V", 5)],
        [("V", 6), ("C", 0), ("C", 1), ("C", 2), ("C", 3)],
        [("C", 4), ("C", 5), ("C", 6)],
        [("K", 0), ("K", 1), ("K", 2)],
        [("K", 3), ("K", 4), ("K", 5)],
        [("K", 6), ("K", 7)],
        [],
    ]
    NW = 7
    SIDE_LAST = [SIDE[0], SIDE[1], [("V", 6), ("W", 0), ("W", 1)], [("W", 2), ("W", 3)],
                 [("W", 4), ("W", 5)], [("W", 6)], [], []]

    def uses(side):
        order = []
        for g in range(G):
            order += [("PT", g, f) for f in range(len(PT_TILES))] + side[g]
        return {item: n for n, item in enumerate(order)}

    USE, USE_LAST = uses(SIDE), uses(SIDE_LAST)
    PER = len(USE)
    FIRST = [("X", 0), ("X", 1), ("Q", 0), ("Q", 1)] + [("C", n) for n in range(NC)] + [("K", n) for n in range(NK)]
    FUSE = {item: n for n, item in enumerate(FIRST)}
    BASE = len(FIRST)

    with ExitStack() as stack:
        def sb(name, shape, dt):
            return stack.enter_context(nc.sbuf_tensor(name, shape, dt))

        def sem(name):
            return stack.enter_context(nc.semaphore(name))

        context = sb("context", [P, KT, D], F32)
        ctxT_hi = sb("ctxT_hi", [P, DH, KPAD], F32R)
        ctxT_lo = sb("ctxT_lo", [P, DH, KPAD], F32R)
        keysT = sb("keysT", [P, 2, DH, KS], F32)
        k_stack = sb("k_stack", [3 * PAIR, G, KS], F32R)
        q_stack = sb("q_stack", [3 * PAIR, G, P], F32R)
        probs = sb("probs", [P, 2, KPAD], F32)
        probsT = sb("probsT", [P, 4, KT, P], F32)
        values = sb("values", [P, KT, D], F32)
        mask_b = sb("mask_b", [P, LK], U8)
        mask_add = sb("mask_add", [P, KS], BF16)
        wk_hi = sb("wk_hi", [P, DH, D], F32R)
        wk_lo = sb("wk_lo", [P, DH, D], F32R)
        wv_hi = sb("wv_hi", [P, DH, D], F32R)
        wv_lo = sb("wv_lo", [P, DH, D], F32R)
        wo = sb("wo", [P, DH, D], F32)
        attnT = sb("attnT", [P, DH, T], F32)
        xres = sb("xres", [P, TJ, D], F32)
        cst = sb("cst", [P, CONSTS], F32)
        cols = sb("cols", [P, 2, DH], F32)
        bv_row = sb("bv_row", [P, 2, D], F32)
        bo_row = sb("bo_row", [P, D], F32)
        xmin = sb("xmin", [P, 2], F32)
        psums = sb("psums", [P, G], F32)
        precip = sb("precip", [P, 4], F32)
        pair_recip = sb("pair_recip", [P, 4, PAIR], F32)
        recipT = sb("recipT", [P, P], F32)
        prod = sb("prod", [P, 2, LQ], F32)
        stats = sb("stats", [P, TJ, 6], F32)
        mv = sb("mv", [P, TJ, 2], F32)
        rstd = sb("rstd", [P, TJ], F32)
        sbv_col = sb("sbv_col", [P, 3, DH], F32)
        sbo_row = sb("sbo_row", [P, D], F32)
        mus = sb("mus", [P, 2, 2, DH], F32)

        ident = cst[:, C_ID:C_ID + P]
        pair_mask = cst[:, C_PAIR:C_PAIR + PAIR]
        head_mask = cst[:, C_HEAD:C_HEAD + H // DH]
        side_mask = cst[:, C_SIDE:C_SIDE + 2]

        flat_pT = probsT[:, :, :, :].rearrange("p a b c -> p (a b c)")
        flat_p = probs[:, :, :].rearrange("p a b -> p (a b)")
        flat_v = values[:, :, :].rearrange("p a b -> p (a b)")
        flat_c = context[:, :, :].rearrange("p a b -> p (a b)")
        flat_k = keysT[:, :, :, :].rearrange("p a b c -> p (a b c)")

        def part(flat, at, *shape):
            size = 1
            for s in shape:
                size *= s
            v = flat[:, at:at + size]
            if len(shape) == 2:
                return v.rearrange("p (a b) -> p a b", b=shape[1])
            if len(shape) == 3:
                return v.rearrange("p (a b c) -> p a b c", b=shape[1], c=shape[2])
            return v.rearrange("p (a b c d) -> p a b c d", b=shape[1], c=shape[2], d=shape[3])

        xn = part(flat_p, 0, TJ, D)
        xnT = part(flat_p, TJ * D, DH, T)
        w_raw = part(flat_v, 0, 3, DH, D)
        qT = part(flat_v, 3 * DH * D, DH, T)
        q_pair = part(flat_pT, 0, DH, B, 2, LQ)
        q_pair_hi = part(flat_pT, DH * T * 2, DH, B, 2, LQ)
        q_pair_lo = part(flat_pT, 2 * DH * T * 2, DH, B, 2, LQ)

        score_banks = stack.enter_context(nc.psum_tensor("score_banks", [P, NCH, 512], F32))
        ring_banks = [stack.enter_context(nc.psum_tensor(f"ring{n}", [P, 512], F32)) for n in range(3)]
        pv_bank = stack.enter_context(nc.psum_tensor("pv_bank", [P, 512], F32))

        q_dram = nc.dram_tensor("q_stacks", (B, 3 * PAIR, G, P), F32, kind="Internal").ap()

        x_loaded = sem("x_loaded")
        w_loaded = sem("w_loaded")
        small_loaded = sem("small_loaded")
        context_loaded = sem("context_loaded")
        mask_loaded = sem("mask_loaded")
        q_stored = sem("q_stored")
        q_first_loaded = sem("q_first_loaded")
        q_second_loaded = sem("q_second_loaded")
        stacked = [sem(f"stacked{g}") for g in range(G)]
        tail_w_loaded = sem("tail_w_loaded")
        out_stored = sem("out_stored")

        dve_step = sem("dve_step")
        act_step = sem("act_step")
        pads_ready = sem("pads_ready")
        xn_ready = sem("xn_ready")
        var_ready = sem("var_ready")
        std_ready = sem("std_ready")
        q_pair_ready = sem("q_pair_ready")
        weights_ready = sem("weights_ready")
        hi_ready = sem("hi_ready")
        mask_ready = sem("mask_ready")
        scores_ready = sem("scores_ready")
        masked_ready = sem("masked_ready")
        probs_ready = sem("probs_ready")
        recip_step = sem("recip_step")
        pair_recip_ready = sem("pair_recip_ready")
        pv_ready = sem("pv_ready")
        prod_ready = sem("prod_ready")
        pv_free = sem("pv_free")
        ring = Ring(ring_banks, [sem(f"filled{n}") for n in range(3)], [sem(f"freed{n}") for n in range(3)], PER)
        tail_banks = [score_banks[:, n, :] for n in range(NCH)] + [r[:, :] for r in ring_banks]
        tring = Ring(tail_banks, [sem(f"tfilled{n}") for n in range(7)], [sem(f"tfreed{n}") for n in range(7)])
        assert PER % 3 == 0

        def use(item, last=False):
            return BASE + (USE_LAST if last else USE)[item]

        TAIL = [("Y", j) for j in range(TJ)] + [("X2", 0), ("X2", 1)]
        TAIL += [("Q2", 0), ("Q2", 1), ("K2", 0), ("K2", 1)] + [("V2", j) for j in range(TJ)]
        for n in range(TJ * DH + 1):
            if n < TJ * DH:
                TAIL.append(("S2", n))
            if n >= 1:
                TAIL.append(("P2", n - 1))
        TAIL += [("O2", 0), ("O2", 1)] + [("Y2", j) for j in range(TJ)] + [("X3", 0), ("X3", 1)]
        TAIL += [("FK", 0), ("FK", 1)] + [("FR", j) for j in range(TJ)] + [("FV", j) for j in range(TJ)]
        TUSE = {item: n for n, item in enumerate(TAIL)}

        w_nat = part(flat_k, 0, NW, DH, D)
        wT6 = part(flat_c, 0, 6, DH, D)
        wT1 = sb("wT1", [P, DH, D], F32)

        def wT(n):
            return wT6[:, n] if n < 6 else wT1

        W_Q, W_K, W_V, W_O, W_FR, W_FK, W_FV = range(NW)

        xn2 = part(flat_p, 0, TJ, D)
        xnT2 = part(flat_p, TJ * D, DH, T)
        q2T = part(flat_v, 0, DH, T)
        k2T = part(flat_v, DH * T, DH, T)
        k2_diag = part(flat_pT, 0, 2, H // DH, LQ)
        p2 = part(flat_pT, 1024, 2, H // DH, LQ)
        p2T = part(flat_pT, 2048, TJ * DH, T)[:, :, :]
        v2 = part(flat_k, 0, B, G, PAIR)
        x3T = part(flat_p, TJ * D, DH, T)
        xprev = part(flat_v, 0, DH, T)
        xrT = part(flat_pT, 0, DH, T)
        xkT = part(flat_pT, DH * T, DH, T)
        kaT = part(flat_pT, 2 * DH * T, DH, T)
        gate = part(flat_pT, 3 * DH * T, TJ, D)
        shifted2_ready = sem("shifted2_ready")
        exp2_ready = sem("exp2_ready")
        diag_ready = sem("diag_ready")
        p2_ready = sem("p2_ready")
        mixed_ready = sem("mixed_ready")
        small2 = sb("small2", [P, 3, H // DH], F32)

        block = stack.enter_context(nc.Block())

        @block.sync
        def _(sp):
            sp.dma_start(xres[:, :, :], x.rearrange("(j b) q d -> (b q) j d", b=2)).then_inc(x_loaded, 16)
            sp.dma_start(cst[:, :], consts).then_inc(x_loaded, 16)

            def load_context(b):
                src = ctx[b] if type(b) is int else \
                    ctx.rearrange("b s d -> (b s d)")[bass.ds(b, LK * D)].rearrange("(s d) -> s d", d=D)
                sp.dma_start(context[:, 0:KT - 1, :],
                             src[0:(KT - 1) * P, :].rearrange("(t p) d -> p t d", p=P)).then_inc(context_loaded, 16)
                sp.dma_start(context[0:KTAIL, KT - 1, :], src[(KT - 1) * P:LK, :]).then_inc(context_loaded, 16)

            def load_mask(b):
                for h2 in range(2):
                    src = mask[b] if type(b) is int else \
                        mask.rearrange("b q s -> (b q s)")[bass.ds(b, LQ * LK)].rearrange("(q s) -> q s", s=LK)
                    sp.dma_start(mask_b[h2 * LQ:(h2 + 1) * LQ, :], src).then_inc(mask_loaded, 16)

            def load_q(b, second):
                lo = second * G // 2
                src = q_dram[b] if type(b) is int else \
                    q_dram.rearrange("b r g c -> (b r g c)")[bass.ds(b, 3 * PAIR * G * P)]\
                    .rearrange("(r g c) -> r g c", g=G, c=P)
                sp.dma_start(q_stack[:, lo:lo + G // 2, :].bitcast(F32), src[:, lo:lo + G // 2, :])\
                  .then_inc(q_second_loaded if second else q_first_loaded, 16)

            def stack_keys(half):
                for p in range(4):
                    g = 4 * half + p
                    for n, which in enumerate((0, 0, 1)):
                        sp.dma_start(k_stack[n * PAIR:(n + 1) * PAIR, g, :].bitcast(F32),
                                     keysT[p * PAIR:(p + 1) * PAIR, which, half, :])\
                          .then_inc(stacked[g], 16)

            for n, w in enumerate((Wq, Wk, Wv)):
                sp.dma_start(w_raw[:, n], w.rearrange("(t p) n -> p t n", p=P)).then_inc(w_loaded, 16)
                if n == 0:
                    load_context(0)
            load_mask(0)
            sp.wait_ge(q_pair_ready, 2)
            for n, src in enumerate((q_pair_hi, q_pair_lo, q_pair_hi)):
                for p in range(4):
                    for half in range(DH):
                        sp.dma_start(
                            q_dram[:, n * PAIR:(n + 1) * PAIR, 4 * half + p, :].rearrange("b r c -> r b c"),
                            src[p * PAIR:(p + 1) * PAIR, half].rearrange("p b h q -> p b (h q)"),
                        ).then_inc(q_stored, 16)
            sp.wait_ge(q_stored, 16 * 3 * 4 * DH)
            load_q(0, 0)
            load_q(0, 1)
            ring.wait_filled(sp, FUSE["C", NC - 1])
            load_context(1)
            for half in range(DH):
                ring.wait_taken(sp, [FUSE["K", half * NCH + n] for n in range(NCH)])
                stack_keys(half)

            def body(b, more):
                def known(v):
                    return v if type(v) is int else sp.snap(v)

                in_loop = type(b) is not int
                mask_at = known((b + 1) * (LQ * LK) if in_loop else b + 1)
                q_at = known((b + 1) * (3 * PAIR * G * P) if in_loop else b + 1)
                context_at = known((b + 2) * (LK * D) if in_loop else b + 2)
                made = known(b + 1)
                half_scored, scored = known(b * G + G // 2), known(b * G + G)
                turns = known(b * ring.turns)
                transposed = known(turns + (use(("C", NC - 1)) // 3 + 1))
                projected = [[(n, known(turns + c)) for n, c in ring.last_fills([use(("K", half * NCH + n)) for n in range(NCH)])]
                             for half in range(DH)]
                sp.wait_ge(mask_ready, made)
                sp.nop(nofuse=True)
                load_mask(mask_at)
                sp.wait_ge(scores_ready, half_scored)
                sp.nop(nofuse=True)
                load_q(q_at, 0)
                if more:
                    sp.wait_ge(ring.filled[use(("C", NC - 1)) % 3], transposed)
                    sp.nop(nofuse=True)
                    load_context(context_at)
                for n, count in projected[0]:
                    sp.wait_ge(ring.freed[n], count)
                    sp.nop(nofuse=True)
                stack_keys(0)
                sp.wait_ge(scores_ready, scored)
                sp.nop(nofuse=True)
                load_q(q_at, 1)
                for n, count in projected[1]:
                    sp.wait_ge(ring.freed[n], count)
                    sp.nop(nofuse=True)
                stack_keys(1)

            with sp.Fori(0, LAST - 1) as b:
                body(b, True)
            body(LAST - 1, False)
            for g in range(G):
                sp.wait_ge(stacked[g], 48 * B)
            for n, w in enumerate((sWq, sWk, sWv, sWo, fWr, fWk, fWv)):
                w = w.rearrange("h d e -> (h d) e") if len(w.shape) == 3 else w
                sp.dma_start(w_nat[:, n], w.rearrange("(t p) n -> p t n", p=P)).then_inc(tail_w_loaded, 16)
            out_t = out.rearrange("(j b) q d -> (b q) j d", b=2)
            for j in range(TJ):
                tring.wait_taken(sp, [TUSE["FV", j]])
                sp.dma_start(out_t[:, j, :], xres[:, j, :]).then_inc(out_stored, 16)
            sp.wait_ge(out_stored, 16 * TJ)

        @block.gpsimd
        def _(pool):
            for n, v in enumerate((bq, bk)):
                pool.dma_start(cols[:, n, :], v.rearrange("(t p) -> p t", p=P),
                               allow_slow_non_contiguous=True).then_inc(small_loaded, 16)
            for n in range(2):
                pool.dma_start(bv_row[:, n, :], bv.rearrange("(a n) -> a n", a=1).broadcast_to([P, D]))\
                    .then_inc(small_loaded, 16)
            pool.dma_start(bo_row[:, :], bo.rearrange("(a n) -> a n", a=1).broadcast_to([P, D])).then_inc(small_loaded, 16)
            pool.dma_start(wo[:, :, :], Wo.rearrange("(t p) n -> p t n", p=P)).then_inc(small_loaded, 16)
            for n, v in enumerate((sbq, sbk, sbv)):
                pool.dma_start(sbv_col[:, n, :], v.rearrange("h d -> (h d)").rearrange("(t p) -> p t", p=P),
                               allow_slow_non_contiguous=True)\
                    .then_inc(small_loaded, 16)
            pool.dma_start(sbo_row[:, :], sbo.rearrange("(a n) -> a n", a=1).broadcast_to([P, D]))\
                .then_inc(small_loaded, 16)
            for n, v in enumerate((mu_r, mu_k)):
                pool.dma_start(mus[:, n, 0, :], v.rearrange("(t p) -> p t", p=P),
                               allow_slow_non_contiguous=True).then_inc(small_loaded, 16)
            pool.memset(ctxT_hi[:, :, LK:KPAD].bitcast(F32), 0.0).then_inc(pads_ready, 1)
            pool.memset(ctxT_lo[:, :, LK:KPAD].bitcast(F32), 0.0).then_inc(pads_ready, 1)
            pool.memset(mask_add[:, LK:KS], PADDED).then_inc(pads_ready, 1)

        SMALL = 16 * 12
        PADS = 3

        @block.scalar
        def _(act):
            def copy(dst, src):
                return nc.scalar.activation(dst, src, ACT.Copy)

            def sqrt_of_variance(n):
                act.wait_ge(var_ready, n)
                nc.scalar.activation(rstd[:, :], rstd[:, :], ACT.Sqrt).then_inc(std_ready, 1)

            def context_hi(n, u, b):
                tiles = min(2, KT - 2 * n)
                width = P * tiles if n < NC - 1 else KTAIL
                ring.wait_filled(act, u, b)
                src = ring.bank(u)[:, :].rearrange("p (t k) -> p t k", t=DH)[:, :, 0:width]
                copy(ctxT_hi[:, :, 2 * n * P:2 * n * P + width], src).then_inc(hi_ready, 1)

            def keys_hi(n, u, b, first=False):
                half, c = divmod(n, NCH)
                ring.wait_filled(act, u, b)
                if c == 0 and not first:
                    for g in range(4 * half, 4 * half + 4):
                        act.wait_ge(stacked[g], (b + 1) * 48)
                nc.scalar.activation(keysT[:, 0, half, c * CH:(c + 1) * CH].bitcast(F32R), ring.bank(u)[:, 0:CH],
                                     ACT.Identity, bias=cols[:, 1, half:half + 1]).then_inc(hi_ready, 1)

            def exps(b, g):
                s = b * G + g
                act.wait_ge(masked_ready, s + 1)
                nc.scalar.activation(probs[:, g % 2, 0:KS], probs[:, g % 2, 0:KS], ACT.Exp,
                                     bias=xmin[:, g % 2:g % 2 + 1], scale=-1.0,
                                     accum_out=psums[:, g:g + 1]).then_inc(probs_ready, 1)

            sqrt_of_variance(1)
            for n in range(2):
                ring.wait_filled(act, FUSE["X", n])
                copy(xnT[:, n, :], ring.bank(FUSE["X", n])[:, :]).then_inc(ring.freed[FUSE["X", n] % 3], 1)
            act.wait_ge(small_loaded, SMALL)
            for n in range(NC):
                context_hi(n, FUSE["C", n], 0)
            for n in range(NK):
                keys_hi(n, FUSE["K", n], 0, first=True)
            exps(0, 0)

            def body(b, last):
                for g in range(G):
                    for f, tiles in enumerate(PT_TILES):
                        u = use(("PT", g, f), last)
                        ring.wait_filled(act, u, b)
                        bank = ring.bank(u)
                        done = copy(probsT[:, g % 4, tiles[0]:tiles[-1] + 1, :],
                                    bank[:, 0:len(tiles) * P].rearrange("p (t c) -> p t c", c=P))
                        if g % 4 == 3 and f == len(PT_TILES) - 1:
                            done = copy(recipT[:, :], bank[:, 3 * P:4 * P])
                        done.then_inc(ring.freed[u % 3], 1)
                    if g < G - 1:
                        exps(b, g + 1)
                    elif not last:
                        exps(b + 1, 0)
                    for kind, n in (SIDE_LAST if last else SIDE)[g]:
                        u = use((kind, n), last)
                        if kind == "C":
                            context_hi(n, u, b)
                        if kind == "W":
                            ring.wait_filled(act, u, b)
                            copy(wT(n)[:, :, :], ring.bank(u)[:, :].rearrange("p (t d) -> p t d", t=DH))\
                                .then_inc(ring.freed[u % 3], 1)
                        if kind == "K":
                            keys_hi(n, u, b)

            with act.Fori(0, LAST) as b:
                body(b, False)
            body(LAST, True)

            def take(item, dst, src=None, func=ACT.Copy, **more):
                u = TUSE[item]
                tring.wait_filled(act, u)
                nc.scalar.activation(dst, tring.bank(u)[:, :] if src is None else src(tring.bank(u)), func, **more)\
                    .then_inc(tring.freed[u % tring.n], 1)

            sqrt_of_variance(2)
            for n in range(2):
                take(("X2", n), xnT2[:, n, :])
            for n in range(DH):
                take(("Q2", n), q2T[:, n, :], func=ACT.Identity, bias=sbv_col[:, 0, n:n + 1])
            for n in range(DH):
                take(("K2", n), k2T[:, n, :], func=ACT.Identity, bias=sbv_col[:, 1, n:n + 1])
            for n in range(TJ * DH):
                act.wait_ge(shifted2_ready, n + 1)
                nc.scalar.activation(p2[:, n % 2], p2[:, n % 2], ACT.Exp, scale=DK ** -0.5).then_inc(exp2_ready, 1)
                if n >= 1:
                    take(("P2", n - 1), p2T[:, n - 1])
            take(("P2", TJ * DH - 1), p2T[:, TJ * DH - 1])
            for n in range(DH):
                take(("O2", n), attnT[:, n, :], func=ACT.Identity, bias=sbv_col[:, 2, n:n + 1])
            sqrt_of_variance(3)
            for n in range(2):
                take(("X3", n), x3T[:, n, :])
            for j in range(TJ):
                take(("FR", j), gate[:, j, :], src=lambda k: k[:, 0:D], func=ACT.Sigmoid)

        @block.vector
        def _(dve):
            steps = [0]

            def link(ins):
                steps[0] += 1
                ins.then_inc(dve_step, 1)
                dve.wait_ge(dve_step, steps[0])

            def layernorm(n, dst):
                for j in range(TJ):
                    last = nc.vector.bn_stats(stats[:, j, :], xres[:, j, :])
                link(last)
                for j in range(TJ):
                    last = nc.vector.bn_aggr(mv[:, j, :], stats[:, j, :])
                link(last)
                nc.vector.tensor_scalar(rstd[:, :], mv[:, :, 1], EPS, None, ALU.add).then_inc(var_ready, 1)
                dve.wait_ge(std_ready, n)
                link(nc.vector.reciprocal(rstd[:, :], rstd[:, :]))
                for j in range(TJ):
                    nc.vector.tensor_scalar(dst[:, j, :], xres[:, j, :], mv[:, j, 0:1], rstd[:, j:j + 1],
                                            ALU.subtract, ALU.mult).then_inc(xn_ready, 1)

            dve.wait_ge(x_loaded, 32)
            layernorm(1, xn)
            dve.wait_ge(w_loaded, 48)
            link(nc.vector.tensor_copy(wk_hi[:, :, :], w_raw[:, 1]))
            nc.vector.tensor_tensor(wk_lo[:, :, :], w_raw[:, 1], wk_hi[:, :, :], ALU.subtract).then_inc(weights_ready, 1)
            dve.wait_ge(small_loaded, SMALL)
            for half in range(DH):
                u = FUSE["Q", half]
                ring.wait_filled(dve, u)
                nc.vector.tensor_scalar(qT[:, half, :], ring.bank(u)[:, :], cols[:, 0, half:half + 1], QSCALE,
                                        ALU.add, ALU.mult).then_inc(ring.freed[u % 3], 1)
            ring.wait_taken(dve, [FUSE["Q", half] for half in range(DH)])
            for h2 in range(2):
                for half in range(DH):
                    last = nc.vector.tensor_scalar(q_pair[:, half, :, h2, :],
                                                   qT[:, half, :].rearrange("p (b q) -> p b q", q=LQ),
                                                   side_mask[:, h2:h2 + 1], None, ALU.mult)
            link(last)
            flat = [v.rearrange("p a b c d -> p (a b c d)") for v in (q_pair, q_pair_hi, q_pair_lo)]
            nc.vector.tensor_copy(flat[1].bitcast(F32R), flat[0]).then_inc(q_pair_ready, 1)
            dve.wait_ge(q_pair_ready, 1)
            nc.vector.tensor_tensor(flat[2].bitcast(F32R), flat[0], flat[1], ALU.subtract).then_inc(q_pair_ready, 1)

            def make_mask(b):
                dve.wait_ge(mask_loaded, (b + 1) * 32)
                nc.vector.tensor_scalar(mask_add[:, 0:LK], mask_b[:, :], MASKED, None, ALU.mult).then_inc(mask_ready, 1)
                dve.wait_ge(mask_ready, b + 1)

            def context_lo(n, u, b, at):
                tiles = min(2, KT - 2 * n)
                width = P * tiles if n < NC - 1 else KTAIL
                dve.wait_ge(hi_ready, at)
                src = ring.bank(u)[:, :].rearrange("p (t k) -> p t k", t=DH)[:, :, 0:width]
                nc.vector.tensor_tensor(ctxT_lo[:, :, 2 * n * P:2 * n * P + width], src,
                                        ctxT_hi[:, :, 2 * n * P:2 * n * P + width], ALU.subtract)\
                    .then_inc(ring.freed[u % 3], 1)

            def keys_lo(n, u, b, at):
                half, c = divmod(n, NCH)
                dve.wait_ge(hi_ready, at)
                nc.vector.scalar_tensor_tensor(
                    out=keysT[:, 1, half, c * CH:(c + 1) * CH].bitcast(F32R), in0=ring.bank(u)[:, 0:CH],
                    scalar=cols[:, 1, half:half + 1], in1=keysT[:, 0, half, c * CH:(c + 1) * CH],
                    op0=ALU.add, op1=ALU.subtract).then_inc(ring.freed[u % 3], 1)

            def mask_scores(b, g):
                dve.wait_ge(scores_ready, b * G + g + 1)
                dve.nop(nofuse=True)
                nc.vector.tensor_tensor_reduce(
                    out=probs[:, g % 2, 0:KS].rearrange("p (n c) -> p n c", n=NCH),
                    in0=score_banks[:, :, 0:CH], in1=mask_add[:, :].rearrange("p (n c) -> p n c", n=NCH),
                    scale=1.0, scalar=3.0e38, op0=ALU.add, op1=ALU.min,
                    accum_out=xmin[:, g % 2:g % 2 + 1]).then_inc(masked_ready, 1)

            HI = NC + NK
            for n in range(NC):
                context_lo(n, FUSE["C", n], 0, n + 1)
            link(nc.vector.tensor_copy(wv_hi[:, :, :], w_raw[:, 2]))
            nc.vector.tensor_tensor(wv_lo[:, :, :], w_raw[:, 2], wv_hi[:, :, :], ALU.subtract).then_inc(weights_ready, 1)
            for n in range(NK):
                keys_lo(n, FUSE["K", n], 0, NC + n + 1)
            for j in range(TJ):
                last = nc.vector.tensor_tensor(xres[:, j, :], xres[:, j, :], bo_row[:, :], ALU.add)
            link(last)
            nc.vector.memset(probs[:, :, KS:KPAD], 0.0).then_inc(pv_free, 1)
            dve.wait_ge(pv_free, 1)
            dve.wait_ge(pads_ready, PADS)
            make_mask(0)
            mask_scores(0, 0)

            def body(b, last):
                made = 0
                for g in range(G):
                    if g < G - 1:
                        mask_scores(b, g + 1)
                    elif not last:
                        make_mask(b + 1)
                        mask_scores(b + 1, 0)
                    for kind, n in (SIDE_LAST if last else SIDE)[g]:
                        u = use((kind, n), last)
                        if kind == "V":
                            ring.wait_filled(dve, u, b)
                            tiles = min(2, KT - 2 * n)
                            nc.vector.tensor_tensor(
                                values[:, 2 * n:2 * n + tiles, :],
                                ring.bank(u)[:, 0:tiles * D].rearrange("p (t d) -> p t d", d=D),
                                bv_row[:, 0:tiles, :], ALU.add).then_inc(ring.freed[u % 3], 1)
                        elif kind in "CK":
                            made += 1
                            (context_lo if kind == "C" else keys_lo)(n, u, b, (b + 1) * HI + made)
                    if g % 4 == 2:
                        h = 2 * b + g // 4
                        dve.wait_ge(probs_ready, b * G + g + 2)
                        nc.vector.reciprocal(precip[:, :], psums[:, g - 2:g + 2]).then_inc(recip_step, 1)
                        dve.wait_ge(recip_step, h + 1)
                        nc.vector.tensor_tensor(
                            pair_recip[:, :, :], precip[:, :].unsqueeze(2).broadcast_to([P, 4, PAIR]),
                            pair_mask.unsqueeze(1).broadcast_to([P, 4, PAIR]), ALU.mult).then_inc(pair_recip_ready, 1)
                    if g % 4 == 3:
                        h = 2 * b + g // 4
                        dve.wait_ge(pv_ready, h + 1)
                        nc.vector.tensor_tensor(prod[:, :, :].rearrange("p h q -> p (h q)"), pv_bank[:, 0:P],
                                                recipT[:, :], ALU.mult).then_inc(prod_ready, 1)
                        dve.wait_ge(prod_ready, h + 1)
                        at = b * LQ
                        dst = attnT[:, g // 4, at:at + LQ] if type(b) is int else attnT[:, g // 4, bass.ds(at, LQ)]
                        nc.vector.tensor_tensor(dst, prod[:, 0, :], prod[:, 1, :], ALU.add).then_inc(pv_free, 1)

            with dve.Fori(0, LAST) as b:
                body(b, False)
            body(LAST, True)

            def bank_of(item):
                u = TUSE[item]
                tring.wait_filled(dve, u)
                return tring.bank(u), tring.freed[u % tring.n]

            for j in range(TJ):
                y, freed = bank_of(("Y", j))
                nc.vector.tensor_tensor(xres[:, j, :], y[:, 0:D], xres[:, j, :], ALU.add).then_inc(freed, 1)
            tring.wait_taken(dve, [TUSE["Y", j] for j in range(TJ)])
            layernorm(2, xn2)
            for j in range(TJ):
                last = nc.vector.tensor_tensor(xres[:, j, :], xres[:, j, :], sbo_row[:, :], ALU.add)
            link(last)
            link(nc.vector.tensor_scalar(mus[:, :, 1, :], mus[:, :, 0, :], -1.0, 1.0, ALU.mult, ALU.add))

            def diag(n):
                j, half = divmod(n, DH)
                for b2 in range(2):
                    m = 2 * n + b2
                    if m >= 2:
                        tring.wait_filled(dve, TUSE["S2", (m - 2) // 2])
                    at = (2 * j + b2) * LQ
                    nc.vector.tensor_tensor(
                        k2_diag[:, m % 2], k2T[:, half, at:at + LQ].unsqueeze(1).broadcast_to([P, H // DH, LQ]),
                        head_mask.unsqueeze(2).broadcast_to([P, H // DH, LQ]), ALU.mult).then_inc(diag_ready, 1)

            for j in range(TJ):
                v, freed = bank_of(("V2", j))
                for b2 in range(2):
                    last = nc.vector.tensor_tensor(
                        v2[:, 2 * j + b2], v[:, b2 * D:(b2 + 1) * D].rearrange("p (g c) -> p g c", c=PAIR),
                        pair_mask.unsqueeze(1).broadcast_to([P, G, PAIR]), ALU.mult)
                last.then_inc(freed, 1)
            tring.wait_taken(dve, [TUSE["K2", 0], TUSE["K2", 1]])
            diag(0)

            def softmax_end(n):
                dve.wait_ge(exp2_ready, n + 1)
                link(nc.vector.tensor_reduce(small2[:, 1, :], p2[:, n % 2], AX.X, ALU.add))
                link(nc.vector.reciprocal(small2[:, 2, :], small2[:, 1, :]))
                nc.vector.tensor_tensor(p2[:, n % 2], p2[:, n % 2],
                                        small2[:, 2, :].unsqueeze(2).broadcast_to([P, H // DH, LQ]),
                                        ALU.mult).then_inc(p2_ready, 1)

            for n in range(TJ * DH):
                if n + 1 < TJ * DH:
                    diag(n + 1)
                s, freed = bank_of(("S2", n))
                s = s[:, :].rearrange("p (h k) -> p h k", k=LQ)
                link(nc.vector.tensor_reduce(small2[:, 0, :], s, AX.X, ALU.max))
                if n >= 2:
                    tring.wait_filled(dve, TUSE["P2", n - 2])
                nc.vector.tensor_tensor(p2[:, n % 2], s,
                                        small2[:, 0, :].unsqueeze(2).broadcast_to([P, H // DH, LQ]),
                                        ALU.subtract).then_inc(freed, 1)
                tring.wait_taken(dve, [TUSE["S2", n]])
                nc.vector.engine_nop().then_inc(shifted2_ready, 1)
                if n >= 1:
                    softmax_end(n - 1)
            softmax_end(TJ * DH - 1)
            for j in range(TJ):
                y, freed = bank_of(("Y2", j))
                nc.vector.tensor_tensor(xres[:, j, :], y[:, 0:D], xres[:, j, :], ALU.add).then_inc(freed, 1)
            tring.wait_taken(dve, [TUSE["Y2", j] for j in range(TJ)])
            layernorm(3, xn2)
            xp = xprev.rearrange("p t (b q) -> p t b q", q=LQ)
            x3 = x3T.rearrange("p t (b q) -> p t b q", q=LQ)
            link(nc.vector.memset(xp[:, :, :, 0:1], 0.0))
            tring.wait_taken(dve, [TUSE["X3", 0], TUSE["X3", 1]])
            for half in range(DH):
                last = nc.vector.tensor_copy(xp[:, half, :, 1:LQ], x3[:, half, :, 0:LQ - 1])
            link(last)
            for n, dst in ((1, xkT), (0, xrT)):
                for half in range(DH):
                    last = nc.vector.tensor_scalar(dst[:, half, :], x3T[:, half, :], mus[:, n, 0, half:half + 1], None, ALU.mult)
                link(last)
                for half in range(DH):
                    nc.vector.scalar_tensor_tensor(
                        out=dst[:, half, :], in0=xprev[:, half, :], scalar=mus[:, n, 1, half:half + 1],
                        in1=dst[:, half, :], op0=ALU.mult, op1=ALU.add).then_inc(mixed_ready, 1)
            for half in range(DH):
                k, freed = bank_of(("FK", half))
                link(nc.vector.tensor_scalar(kaT[:, half, :], k[:, :], 0.0, None, ALU.max))
                nc.vector.tensor_tensor(kaT[:, half, :], kaT[:, half, :], kaT[:, half, :], ALU.mult).then_inc(freed, 1)
            for j in range(TJ):
                tring.wait_taken(dve, [TUSE["FR", j]])
                v, freed = bank_of(("FV", j))
                link(nc.vector.tensor_tensor(gate[:, j, :], v[:, 0:D], gate[:, j, :], ALU.mult))
                nc.vector.tensor_tensor(xres[:, j, :], gate[:, j, :], xres[:, j, :], ALU.add).then_inc(freed, 1)

        @block.tensor
        def _(pe):
            def transposes(dst, srcs):
                for n, src in enumerate(srcs):
                    rows, width = src.shape[0], src.shape[1]
                    last = nc.tensor.transpose(dst[0:width, n * P:n * P + rows], src, ident[0:rows, 0:rows])
                return last

            def three_passes(dst, terms):
                terms = [t for ah, al, bh, bl in terms for t in ((ah, bh), (al, bh), (ah, bl))]
                for n, (a, c) in enumerate(terms):
                    last = nc.tensor.matmul(dst, a, c, start=(n == 0), stop=(n == len(terms) - 1))
                return last

            def context_transposes(n, u, b, wait):
                ring.wait_free(pe, u, b)
                if n == 0:
                    pe.wait_ge(context_loaded, wait)
                bank = ring.bank(u)
                for half in range(DH):
                    for t in range(2 * n, min(2 * n + 2, KT)):
                        rows = P if t < KT - 1 else KTAIL
                        at = half * 2 * P + (t - 2 * n) * P
                        last = nc.tensor.transpose(bank[:, at:at + rows],
                                                   context[0:rows, t, half * P:(half + 1) * P], ident[0:rows, 0:rows])
                last.then_inc(ring.filled[u % 3], 1)

            def project_keys(n, u, b, first):
                half, c = divmod(n, NCH)
                ring.wait_free(pe, u, b)
                cs = slice(half * P, (half + 1) * P)
                ks = slice(c * CH, (c + 1) * CH)
                three_passes(ring.bank(u)[:, 0:CH],
                             [(wk_hi[:, t, cs], wk_lo[:, t, cs], ctxT_hi[:, t, ks], ctxT_lo[:, t, ks])
                              for t in range(DH)]).then_inc(ring.filled[u % 3], 1)

            def project_values(n, u, b):
                ring.wait_free(pe, u, b)
                for i, t in enumerate(range(2 * n, min(2 * n + 2, KT))):
                    ks = slice(t * P, (t + 1) * P)
                    last = three_passes(ring.bank(u)[:, i * D:(i + 1) * D],
                                        [(ctxT_hi[:, d, ks], ctxT_lo[:, d, ks], wv_hi[:, d, :], wv_lo[:, d, :])
                                         for d in range(DH)])
                last.then_inc(ring.filled[u % 3], 1)

            def scores(b, g):
                if type(b) is not int or b * G + g > 0:
                    pe.wait_ge(masked_ready, b * G + g)
                if g % 4 == 0:
                    pe.wait_ge(q_second_loaded if g else q_first_loaded, (b + 1) * 16)
                pe.wait_ge(stacked[g], (b + 1) * 48)
                for c in range(NCH):
                    last = nc.tensor.matmul(score_banks[:, c, 0:CH], q_stack[:, g, :],
                                            k_stack[:, g, c * CH:(c + 1) * CH], start=True, stop=True)
                last.then_inc(scores_ready, 1)

            for half in range(DH):
                u = FUSE["X", half]
                pe.wait_ge(xn_ready, TJ)
                transposes(ring.bank(u), [xn[:, j, half * P:(half + 1) * P] for j in range(TJ)])\
                    .then_inc(ring.filled[u % 3], 1)
            ring.wait_taken(pe, [FUSE["X", half] for half in range(DH)])
            pe.wait_ge(w_loaded, 48)
            for half in range(DH):
                u = FUSE["Q", half]
                ring.wait_free(pe, u)
                for t in range(DH):
                    last = nc.tensor.matmul(ring.bank(u)[:, :], w_raw[:, 0, t, half * P:(half + 1) * P],
                                            xnT[:, t, :], start=(t == 0), stop=(t == DH - 1))
                last.then_inc(ring.filled[u % 3], 1)
            for n in range(NC):
                context_transposes(n, FUSE["C", n], 0, 32)
            pe.wait_ge(weights_ready, 1)
            pe.wait_ge(pads_ready, PADS)
            ring.wait_taken(pe, [FUSE["C", n] for n in range(NC)])
            for n in range(NK):
                project_keys(n, FUSE["K", n], 0, True)
            scores(0, 0)
            pe.wait_ge(weights_ready, 2)

            def body(b, last_batch):
                for g in range(G):
                    if g < G - 1:
                        scores(b, g + 1)
                    elif not last_batch:
                        scores(b + 1, 0)
                    pe.wait_ge(probs_ready, b * G + g + 1)
                    for f, tiles in enumerate(PT_TILES):
                        u = use(("PT", g, f), last_batch)
                        ring.wait_free(pe, u, b)
                        srcs = [probs[:, g % 2, t * P:(t + 1) * P] for t in tiles]
                        if g % 4 == 3 and f == len(PT_TILES) - 1:
                            pe.wait_ge(pair_recip_ready, 2 * b + g // 4 + 1)
                            srcs.append(pair_recip[:, :, :].rearrange("p a b -> p (a b)"))
                        transposes(ring.bank(u), srcs).then_inc(ring.filled[u % 3], 1)
                    for kind, n in (SIDE_LAST if last_batch else SIDE)[g]:
                        u = use((kind, n), last_batch)
                        if kind == "V":
                            project_values(n, u, b)
                        elif kind == "C":
                            context_transposes(n, u, b, (b + 2) * 32)
                        elif kind == "W":
                            ring.wait_free(pe, u, b)
                            if n == 0:
                                pe.wait_ge(tail_w_loaded, 16 * NW)
                            for half in range(DH):
                                for t in range(DH):
                                    at = half * D + t * P
                                    last = nc.tensor.transpose(ring.bank(u)[:, at:at + P],
                                                               w_nat[:, n, t, half * P:(half + 1) * P], ident)
                            last.then_inc(ring.filled[u % 3], 1)
                        else:
                            if n == 0:
                                ring.wait_taken(pe, [use(("C", m)) for m in range(NC)], b)
                            project_keys(n, u, b, False)
                    if g % 4 == 3:
                        need = [use(("PT", i, f), last_batch) for i in range(g - 3, g + 1) for f in range(len(PT_TILES))]
                        if g == 3:
                            need = [use(("V", n), last_batch) for n in range(NV)] + need
                        pe.wait_ge(pv_free, 2 * b + g // 4 + 1)
                        ring.wait_taken(pe, need, b)
                        for t in range(KT):
                            for p in range(4):
                                ch = (g - 3 + p) * PAIR
                                last = nc.tensor.matmul(pv_bank[p * PAIR:(p + 1) * PAIR, 0:P],
                                                        values[:, t, ch:ch + PAIR], probsT[:, p, t, :],
                                                        start=(t == 0), stop=(t == KT - 1))
                        last.then_inc(pv_ready, 1)

            with pe.Fori(0, LAST) as b:
                body(b, False)
            body(LAST, True)

            def fill(item, dst, terms):
                u = TUSE[item]
                for n, (a, c) in enumerate(terms):
                    last = nc.tensor.matmul(dst, a, c, start=(n == 0), stop=(n == len(terms) - 1))
                return last

            def begin(item):
                u = TUSE[item]
                tring.wait_free(pe, u)
                return tring.bank(u), tring.filled[u % tring.n]

            ring.wait_taken(pe, [use(("PT", G - 1, f), True) for f in range(len(PT_TILES))] + [use(("W", NW - 1), True)], LAST)
            pe.wait_ge(masked_ready, B * G)
            pe.wait_ge(pv_free, 2 * B + 1)
            for j in range(TJ):
                k, filled = begin(("Y", j))
                fill(("Y", j), k[:, 0:D], [(attnT[:, t, j * P:(j + 1) * P], wo[:, t, :]) for t in range(DH)])\
                    .then_inc(filled, 1)
            pe.wait_ge(xn_ready, 2 * TJ)
            for half in range(DH):
                k, filled = begin(("X2", half))
                transposes(k, [xn2[:, j, half * P:(half + 1) * P] for j in range(TJ)]).then_inc(filled, 1)
            tring.wait_taken(pe, [TUSE["X2", 0], TUSE["X2", 1]])
            for name, w in (("Q2", W_Q), ("K2", W_K)):
                for half in range(DH):
                    k, filled = begin((name, half))
                    fill((name, half), k[:, :], [(wT(w)[:, t, half * P:(half + 1) * P], xnT2[:, t, :]) for t in range(DH)])\
                        .then_inc(filled, 1)
            for j in range(TJ):
                k, filled = begin(("V2", j))
                for b2 in range(2):
                    at = (2 * j + b2) * LQ
                    for t in range(DH):
                        for h2 in range(2):
                            last = nc.tensor.matmul(k[h2 * LQ:(h2 + 1) * LQ, b2 * D:(b2 + 1) * D],
                                                    xnT2[:, t, at:at + LQ], wT(W_V)[:, t, :],
                                                    start=(t == 0), stop=(t == DH - 1), skip_group_check=True)
                last.then_inc(filled, 1)
            tring.wait_taken(pe, [TUSE["Q2", 0], TUSE["Q2", 1], TUSE["K2", 0], TUSE["K2", 1]])

            def transpose_p2(n):
                k, filled = begin(("P2", n))
                pe.wait_ge(p2_ready, n + 1)
                flat = p2[:, n % 2].rearrange("p h k -> p (h k)")
                transposes(k, [flat[:, i * P:(i + 1) * P] for i in range(4)]).then_inc(filled, 1)

            for n in range(TJ * DH):
                j, half = divmod(n, DH)
                k, filled = begin(("S2", n))
                pe.wait_ge(diag_ready, 2 * n + 2)
                for b2 in range(2):
                    at = (2 * j + b2) * LQ
                    last = nc.tensor.matmul(k[b2 * LQ:(b2 + 1) * LQ, :], q2T[:, half, at:at + LQ],
                                            k2_diag[:, b2].rearrange("p h k -> p (h k)"), start=True, stop=True)
                last.then_inc(filled, 1)
                if n >= 1:
                    transpose_p2(n - 1)
            transpose_p2(TJ * DH - 1)
            tring.wait_taken(pe, [TUSE["V2", j] for j in range(TJ)] + [TUSE["P2", n] for n in range(TJ * DH)])
            for half in range(DH):
                k, filled = begin(("O2", half))
                for b in range(B):
                    j, b2 = divmod(b, 2)
                    pT = p2T[:, j * DH + half].rearrange("p (g c) -> p g c", c=P)
                    for p in range(4):
                        last = nc.tensor.matmul(k[p * PAIR:(p + 1) * PAIR, b * LQ:(b + 1) * LQ],
                                                v2[:, b, 4 * half + p, :], pT[:, p, b2 * LQ:(b2 + 1) * LQ],
                                                start=True, stop=True, skip_group_check=True)
                last.then_inc(filled, 1)
            tring.wait_taken(pe, [TUSE["O2", 0], TUSE["O2", 1]])
            for j in range(TJ):
                k, filled = begin(("Y2", j))
                fill(("Y2", j), k[:, 0:D], [(attnT[:, t, j * P:(j + 1) * P], wT(W_O)[:, t, :]) for t in range(DH)])\
                    .then_inc(filled, 1)
            pe.wait_ge(xn_ready, 3 * TJ)
            for half in range(DH):
                k, filled = begin(("X3", half))
                transposes(k, [xn2[:, j, half * P:(half + 1) * P] for j in range(TJ)]).then_inc(filled, 1)
            pe.wait_ge(mixed_ready, 2)
            for half in range(DH):
                k, filled = begin(("FK", half))
                fill(("FK", half), k[:, :], [(wT(W_FK)[:, t, half * P:(half + 1) * P], xkT[:, t, :]) for t in range(DH)])\
                    .then_inc(filled, 1)
            pe.wait_ge(mixed_ready, 4)
            for j in range(TJ):
                k, filled = begin(("FR", j))
                fill(("FR", j), k[:, 0:D], [(xrT[:, t, j * P:(j + 1) * P], wT(W_FR)[:, t, :]) for t in range(DH)])\
                    .then_inc(filled, 1)
            tring.wait_taken(pe, [TUSE["FK", 0], TUSE["FK", 1]])
            for j in range(TJ):
                k, filled = begin(("FV", j))
                fill(("FV", j), k[:, 0:D], [(kaT[:, t, j * P:(j + 1) * P], wT(W_FV)[:, t, :]) for t in range(DH)])\
                    .then_inc(filled, 1)


_INS = ["x", "ctx_1024", "mask_BxSxS2_bf0",
        "L0_xattn_Wq", "L0_xattn_bq", "L0_xattn_Wk", "L0_xattn_bk", "L0_xattn_Wv", "L0_xattn_bv",
        "L0_xattn_Wo", "L0_xattn_bo",
        "L0_attn_Wq", "L0_attn_bq", "L0_attn_Wk", "L0_attn_bk", "L0_attn_Wv", "L0_attn_bv",
        "L0_attn_Wo", "L0_attn_bo",
        "L0_ffn_W_r", "L0_ffn_W_k", "L0_ffn_W_v", "L0_ffn_mu_r", "L0_ffn_mu_k"]


def shape_constants(np):
    c = np.zeros((P, CONSTS), np.float32)
    row = np.arange(P)
    c[:, C_ID:C_ID + P] = np.eye(P, dtype=np.float32)
    c[:, C_PAIR:C_PAIR + 32] = (row[:, None] // 64) == (np.arange(32)[None, :] // 16)
    c[:, C_HEAD:C_HEAD + 8] = (row[:, None] // 16) == np.arange(8)[None, :]
    c[:, C_SIDE:C_SIDE + 2] = (row[:, None] // 16) % 2 == np.arange(2)[None, :]
    return c


def kernel(**inputs):
    import numpy as _np
    import concourse.bacc as _bacc
    from concourse import mybir as _mybir
    from concourse.bass_utils import run_bass_kernel_spmd as _run

    nc = _bacc.Bacc("TRN2", target_bir_lowering=False, num_devices=1)
    arrays, args = {}, []
    for name in _INS:
        a = _np.ascontiguousarray(inputs[name])
        arrays[f"in_{name}_dram"] = a
        args.append(nc.dram_tensor(f"in_{name}_dram", a.shape, _mybir.dt.from_np(a.dtype), kind="ExternalInput").ap())
    a = shape_constants(_np)
    arrays["in_consts_dram"] = a
    args.append(nc.dram_tensor("in_consts_dram", a.shape, _mybir.dt.from_np(a.dtype), kind="ExternalInput").ap())
    args.append(nc.dram_tensor("out_0_dram", (8, 64, 256), _mybir.dt.float32, kind="ExternalOutput").ap())
    perceiver_layer(nc, *args)
    r = _run(nc, [arrays], core_ids=[0])
    return r.results[0]["out_0_dram"]
```

```python
import concourse.bass as bass
from concourse import mybir
from contextlib import ExitStack

F32 = mybir.dt.float32
F32R = mybir.dt.float32r
BF16 = mybir.dt.bfloat16
I32 = mybir.dt.int32
U8 = mybir.dt.uint8
ALU = mybir.AluOpType
ACT = mybir.ActivationFunctionType
AX = mybir.AxisListType

P = 128

C_ID, C_PAIR, C_HEAD, C_SIDE = 0, 128, 160, 168
CONSTS = 176


class Ring:

    def __init__(self, banks, filled, freed, per_batch=0):
        self.banks, self.filled, self.freed = banks, filled, freed
        self.n, self.turns = len(banks), per_batch // len(banks)

    def bank(self, u):
        return self.banks[u % self.n]

    def count(self, u, batch):
        return batch * self.turns + u // self.n if self.turns else u // self.n

    def wait_free(self, eng, u, batch=0):
        if u >= self.n:
            eng.wait_ge(self.freed[u % self.n], self.count(u, batch))

    def wait_filled(self, eng, u, batch=0):
        eng.wait_ge(self.filled[u % self.n], self.count(u, batch) + 1)

    def last_fills(self, us):
        last = {}
        for u in us:
            last[u % self.n] = u
        return [(n, u // self.n + 1) for n, u in last.items()]

    def wait_taken(self, eng, us, batch=0):
        for n, count in self.last_fills(us):
            eng.wait_ge(self.freed[n], batch * self.turns + count if self.turns else count)


def perceiver_layer(
    nc, x, ctx, mask, Wq, bq, Wk, bk, Wv, bv, Wo, bo,
    sWq, sbq, sWk, sbk, sWv, sbv, sWo, sbo, fWr, fWk, fWv, mu_r, mu_k, consts, out,
):
    B, LQ, D = x.shape
    LK = ctx.shape[1]
    H = 16
    DK = D // H
    DH = D // P
    G = H // 2
    PAIR = 2 * DK
    KT = -(-LK // P)
    KTAIL = LK - (KT - 1) * P
    KPAD = KT * P
    CH = 402
    NCH = 4
    KS = NCH * CH
    T = B * LQ
    TJ = T // P
    LAST = B - 1
    QSCALE = -1.0 / DK ** 0.5
    MASKED = 2.0 ** 60
    PADDED = 2.0 ** 100
    EPS = 1e-5
    RSQRT_SEED = 0x5F3759DF
    assert T % P == 0 and KS >= LK and CH % 2 == 0 and 2 * LQ == P

    PT_TILES = [range(0, 4), range(4, 7), range(7, 10), range(10, 13)]
    NV = NC = (KT + 1) // 2
    NK = DH * NCH
    SIDE = [
        [("V", 0), ("V", 1), ("V", 2)],
        [("V", 3), ("V", 4), ("V", 5)],
        [("V", 6), ("C", 0), ("C", 1), ("C", 2), ("C", 3)],
        [("C", 4), ("C", 5), ("C", 6)],
        [("K", 0), ("K", 1), ("K", 2)],
        [("K", 3), ("K", 4), ("K", 5)],
        [("K", 6), ("K", 7)],
        [],
    ]
    NW = 7
    SIDE_LAST = [
        SIDE[0],
        SIDE[1],
        [("V", 6), ("W", 0), ("W", 1)],
        [("Y", 0), ("Y", 1), ("Y", 2), ("W", 2)],
        [("W", 3), ("W", 4), ("W", 5)],
        [("W", 6), ("X", 0), ("X", 1)],
        [("X", 2), ("QK", 0)],
        [("QK", 1), ("QK", 2)],
    ]
    EARLY = TJ - 1

    def uses(side):
        order = []
        for g in range(G):
            order += [("PT", g, f) for f in range(len(PT_TILES))] + side[g]
        return {item: n for n, item in enumerate(order)}

    USE, USE_LAST = uses(SIDE), uses(SIDE_LAST)
    PER = len(USE)
    FIRST = [("X", 0), ("X", 1), ("Q", 0), ("Q", 1)] + [("C", n) for n in range(NC)] + [("K", n) for n in range(NK)]
    FUSE = {item: n for n, item in enumerate(FIRST)}
    BASE = len(FIRST)

    STAGES = ["Y", "X", "QK", "V", "S0", "S1", "T0", "T1", "O", "OT", "Y2", "X3", "F", "FV"]
    SKEW = [0, 1, 2, 3]
    TAIL = sorted(((n, j) for n in range(len(STAGES)) for j in range(TJ) if j >= EARLY or n >= 3),
                  key=lambda nj: (nj[0] + SKEW[nj[1]], nj[1]))
    TAIL = [(STAGES[n], j) for n, j in TAIL]
    TUSE = {item: n for n, item in enumerate(TAIL)}

    with ExitStack() as stack:
        def sb(name, shape, dt):
            return stack.enter_context(nc.sbuf_tensor(name, shape, dt))

        def sem(name):
            return stack.enter_context(nc.semaphore(name))

        context = sb("context", [P, KT, D], F32)
        ctxT_hi = sb("ctxT_hi", [P, DH, KPAD], F32R)
        ctxT_lo = sb("ctxT_lo", [P, DH, KPAD], F32R)
        keysT = sb("keysT", [P, 2, DH, KS], F32)
        k_stack = sb("k_stack", [3 * PAIR, G, KS], F32R)
        q_stack = sb("q_stack", [3 * PAIR, G, P], F32R)
        probs = sb("probs", [P, 2, KPAD], F32)
        probsT = sb("probsT", [P, 4, KT, P], F32)
        values = sb("values", [P, KT, D], F32)
        mask_b = sb("mask_b", [P, LK], U8)
        mask_add = sb("mask_add", [P, KS], BF16)
        wk_hi = sb("wk_hi", [P, DH, D], F32R)
        wk_lo = sb("wk_lo", [P, DH, D], F32R)
        wv_hi = sb("wv_hi", [P, DH, D], F32R)
        wv_lo = sb("wv_lo", [P, DH, D], F32R)
        wo = sb("wo", [P, DH, D], F32)
        attnT = sb("attnT", [P, DH, T], F32)
        xres = sb("xres", [P, TJ, D], F32)
        cst = sb("cst", [P, CONSTS], F32)
        cols = sb("cols", [P, 2, DH], F32)
        bv_row = sb("bv_row", [P, 2, D], F32)
        bo_row = sb("bo_row", [P, D], F32)
        xmin = sb("xmin", [P, 2], F32)
        psums = sb("psums", [P, G], F32)
        precip = sb("precip", [P, 4], F32)
        pair_recip = sb("pair_recip", [P, 4, PAIR], F32)
        recipT = sb("recipT", [P, P], F32)
        prod = sb("prod", [P, 2, LQ], F32)
        stats = sb("stats", [P, TJ, 6], F32)
        mv = sb("mv", [P, TJ, 2], F32)
        rstd = sb("rstd", [P, TJ], F32)
        newton = sb("newton", [P, 5, TJ], F32)
        newton_bits = sb("newton_bits", [P, 1, TJ], I32)
        sbv_col = sb("sbv_col", [P, 3, DH], F32)
        sbo_row = sb("sbo_row", [P, D], F32)
        mus = sb("mus", [P, 2, 2, DH], F32)

        ident = cst[:, C_ID:C_ID + P]
        pair_mask = cst[:, C_PAIR:C_PAIR + PAIR]
        head_mask = cst[:, C_HEAD:C_HEAD + H // DH]
        side_mask = cst[:, C_SIDE:C_SIDE + 2]

        flat_pT = probsT[:, :, :, :].rearrange("p a b c -> p (a b c)")
        flat_p = probs[:, :, :].rearrange("p a b -> p (a b)")
        flat_v = values[:, :, :].rearrange("p a b -> p (a b)")
        flat_c = context[:, :, :].rearrange("p a b -> p (a b)")
        flat_k = keysT[:, :, :, :].rearrange("p a b c -> p (a b c)")

        def part(flat, at, *shape):
            size = 1
            for s in shape:
                size *= s
            v = flat[:, at:at + size]
            if len(shape) == 2:
                return v.rearrange("p (a b) -> p a b", b=shape[1])
            if len(shape) == 3:
                return v.rearrange("p (a b c) -> p a b c", b=shape[1], c=shape[2])
            return v.rearrange("p (a b c d) -> p a b c d", b=shape[1], c=shape[2], d=shape[3])

        xn = part(flat_p, 0, TJ, D)
        xnT = part(flat_p, TJ * D, DH, T)
        w_raw = part(flat_v, 0, 3, DH, D)
        qT = part(flat_v, 3 * DH * D, DH, T)
        q_pair = part(flat_pT, 0, DH, B, 2, LQ)
        q_pair_hi = part(flat_pT, DH * T * 2, DH, B, 2, LQ)
        q_pair_lo = part(flat_pT, 2 * DH * T * 2, DH, B, 2, LQ)

        score_banks = stack.enter_context(nc.psum_tensor("score_banks", [P, NCH, 512], F32))
        ring_banks = [stack.enter_context(nc.psum_tensor(f"ring{n}", [P, 512], F32)) for n in range(3)]
        pv_bank = stack.enter_context(nc.psum_tensor("pv_bank", [P, 512], F32))

        q_dram = nc.dram_tensor("q_stacks", (B, 3 * PAIR, G, P), F32, kind="Internal").ap()

        x_loaded = sem("x_loaded")
        w_loaded = sem("w_loaded")
        small_loaded = sem("small_loaded")
        context_loaded = sem("context_loaded")
        mask_loaded = sem("mask_loaded")
        q_stored = sem("q_stored")
        q_first_loaded = sem("q_first_loaded")
        q_second_loaded = sem("q_second_loaded")
        stacked = [sem(f"stacked{g}") for g in range(G)]
        tail_w_loaded = sem("tail_w_loaded")
        out_stored = sem("out_stored")

        dve_step = sem("dve_step")
        act_step = sem("act_step")
        pads_ready = sem("pads_ready")
        xn_ready = sem("xn_ready")
        q_pair_ready = sem("q_pair_ready")
        weights_ready = sem("weights_ready")
        hi_ready = sem("hi_ready")
        mask_ready = sem("mask_ready")
        scores_ready = sem("scores_ready")
        masked_ready = sem("masked_ready")
        probs_ready = sem("probs_ready")
        recip_step = sem("recip_step")
        pair_recip_ready = sem("pair_recip_ready")
        pv_ready = sem("pv_ready")
        prod_ready = sem("prod_ready")
        pv_free = sem("pv_free")
        ring = Ring(ring_banks, [sem(f"filled{n}") for n in range(3)], [sem(f"freed{n}") for n in range(3)], PER)
        tail_banks = [score_banks[:, n, :] for n in range(NCH)] + [r[:, :] for r in ring_banks] + [pv_bank[:, :]]
        tring = Ring(tail_banks, [sem(f"tfilled{n}") for n in range(8)], [sem(f"tfreed{n}") for n in range(8)])
        assert PER % 3 == 0

        def use(item, last=False):
            return BASE + (USE_LAST if last else USE)[item]

        w_nat = part(flat_k, 0, NW, DH, D)
        wT6 = part(flat_c, 0, 6, DH, D)
        wT1 = sb("wT1", [P, DH, D], F32)

        def wT(n):
            return wT6[:, n] if n < 6 else wT1

        W_Q, W_K, W_V, W_O, W_FR, W_FK, W_FV = range(NW)

        HH = H // DH
        VW = DK + 1
        at_k = NW * DH * D
        xn2 = part(flat_k, at_k, TJ, D)
        xnT2 = part(flat_k, at_k + TJ * D, TJ, DH, P)
        q2T = part(flat_k, 0, TJ, DH, P)
        k2T = part(flat_k, TJ * D, TJ, DH, P)
        xrT = part(flat_k, 2 * TJ * D, TJ, DH, P)
        xkT = part(flat_p, TJ * 2 * D, TJ, DH, P)
        k2_diag = part(flat_pT, 0, 2 * DH * 2, HH, LQ)
        p2T = part(flat_pT, 2 * DH * 2 * HH * LQ, 2 * DH, 4, P)
        p2 = part(flat_p, 0, 2 * DH, HH, LQ)
        v2 = part(flat_v, 0, TJ * 2, G, 2 * VW)
        o2 = part(flat_v, TJ * 2 * G * 2 * VW, TJ, D)
        kaT, gate = xnT2, xn2
        xn2_ready = sem("xn2_ready")
        diag_ready = [sem("diag_ready0"), sem("diag_ready1")]
        ones_ready = sem("ones_ready")
        bias_added = sem("bias_added")
        p2_ready = [sem("p2_ready0"), sem("p2_ready1")]
        xn3_ready = sem("xn3_ready")
        scaled_ready = sem("scaled_ready")
        relu_ready = sem("relu_ready")
        ka_ready = sem("ka_ready")
        sum_ready = sem("sum_ready")
        def wait_qk(eng, j):
            if j < EARLY:
                ring.wait_taken(eng, [use(("QK", j), True)], LAST)
            else:
                tring.wait_taken(eng, [TUSE["QK", j]])

        max2 = sb("max2", [P, TJ, DH, HH], F32)
        recip2 = sb("recip2", [P, TJ, H], F32)

        block = stack.enter_context(nc.Block())

        @block.sync
        def _(sp):
            sp.dma_start(xres[:, :, :], x.rearrange("(j b) q d -> (b q) j d", b=2)).then_inc(x_loaded, 16)
            sp.dma_start(cst[:, :], consts).then_inc(x_loaded, 16)

            def load_context(b):
                src = ctx[b] if type(b) is int else \
                    ctx.rearrange("b s d -> (b s d)")[bass.ds(b, LK * D)].rearrange("(s d) -> s d", d=D)
                sp.dma_start(context[:, 0:KT - 1, :],
                             src[0:(KT - 1) * P, :].rearrange("(t p) d -> p t d", p=P)).then_inc(context_loaded, 16)
                sp.dma_start(context[0:KTAIL, KT - 1, :], src[(KT - 1) * P:LK, :]).then_inc(context_loaded, 16)

            def load_mask(b):
                for h2 in range(2):
                    src = mask[b] if type(b) is int else \
                        mask.rearrange("b q s -> (b q s)")[bass.ds(b, LQ * LK)].rearrange("(q s) -> q s", s=LK)
                    sp.dma_start(mask_b[h2 * LQ:(h2 + 1) * LQ, :], src).then_inc(mask_loaded, 16)

            def load_q(b, second):
                lo = second * G // 2
                src = q_dram[b] if type(b) is int else \
                    q_dram.rearrange("b r g c -> (b r g c)")[bass.ds(b, 3 * PAIR * G * P)]\
                    .rearrange("(r g c) -> r g c", g=G, c=P)
                sp.dma_start(q_stack[:, lo:lo + G // 2, :].bitcast(F32), src[:, lo:lo + G // 2, :])\
                  .then_inc(q_second_loaded if second else q_first_loaded, 16)

            def stack_keys(half):
                for p in range(4):
                    g = 4 * half + p
                    for n, which in enumerate((0, 0, 1)):
                        sp.dma_start(k_stack[n * PAIR:(n + 1) * PAIR, g, :].bitcast(F32),
                                     keysT[p * PAIR:(p + 1) * PAIR, which, half, :])\
                          .then_inc(stacked[g], 16)

            for n, w in enumerate((Wq, Wk, Wv)):
                sp.dma_start(w_raw[:, n], w.rearrange("(t p) n -> p t n", p=P)).then_inc(w_loaded, 16)
                if n == 0:
                    load_context(0)
            load_mask(0)
            sp.wait_ge(q_pair_ready, 2)
            for n, src in enumerate((q_pair_hi, q_pair_lo, q_pair_hi)):
                for p in range(4):
                    for half in range(DH):
                        sp.dma_start(
                            q_dram[:, n * PAIR:(n + 1) * PAIR, 4 * half + p, :].rearrange("b r c -> r b c"),
                            src[p * PAIR:(p + 1) * PAIR, half].rearrange("p b h q -> p b (h q)"),
                        ).then_inc(q_stored, 16)
            sp.wait_ge(q_stored, 16 * 3 * 4 * DH)
            load_q(0, 0)
            load_q(0, 1)
            ring.wait_filled(sp, FUSE["C", NC - 1])
            load_context(1)
            for half in range(DH):
                ring.wait_taken(sp, [FUSE["K", half * NCH + n] for n in range(NCH)])
                stack_keys(half)

            def body(b, more):
                def known(v):
                    return v if type(v) is int else sp.snap(v)

                in_loop = type(b) is not int
                mask_at = known((b + 1) * (LQ * LK) if in_loop else b + 1)
                q_at = known((b + 1) * (3 * PAIR * G * P) if in_loop else b + 1)
                context_at = known((b + 2) * (LK * D) if in_loop else b + 2)
                made = known(b + 1)
                half_scored, scored = known(b * G + G // 2), known(b * G + G)
                turns = known(b * ring.turns)
                transposed = known(turns + (use(("C", NC - 1)) // 3 + 1))
                projected = [[(n, known(turns + c)) for n, c in ring.last_fills([use(("K", half * NCH + n)) for n in range(NCH)])]
                             for half in range(DH)]
                sp.wait_ge(mask_ready, made)
                sp.nop(nofuse=True)
                load_mask(mask_at)
                sp.wait_ge(scores_ready, half_scored)
                sp.nop(nofuse=True)
                load_q(q_at, 0)
                if more:
                    sp.wait_ge(ring.filled[use(("C", NC - 1)) % 3], transposed)
                    sp.nop(nofuse=True)
                    load_context(context_at)
                for n, count in projected[0]:
                    sp.wait_ge(ring.freed[n], count)
                    sp.nop(nofuse=True)
                stack_keys(0)
                sp.wait_ge(scores_ready, scored)
                sp.nop(nofuse=True)
                load_q(q_at, 1)
                for n, count in projected[1]:
                    sp.wait_ge(ring.freed[n], count)
                    sp.nop(nofuse=True)
                stack_keys(1)

            with sp.Fori(0, LAST - 1) as b:
                body(b, True)
            body(LAST - 1, False)
            for g in range(G):
                sp.wait_ge(stacked[g], 48 * B)
            for n, w in enumerate((sWq, sWk, sWv, sWo, fWr, fWk, fWv)):
                w = w.rearrange("h d e -> (h d) e") if len(w.shape) == 3 else w
                sp.dma_start(w_nat[:, n], w.rearrange("(t p) n -> p t n", p=P)).then_inc(tail_w_loaded, 16)
            out_t = out.rearrange("(j b) q d -> (b q) j d", b=2)
            for j in range(TJ):
                sp.wait_ge(sum_ready, j + 1)
                sp.dma_start(out_t[:, j, :], xres[:, j, :]).then_inc(out_stored, 16)
            sp.wait_ge(out_stored, 16 * TJ)

        @block.gpsimd
        def _(pool):
            for n, v in enumerate((bq, bk)):
                pool.dma_start(cols[:, n, :], v.rearrange("(t p) -> p t", p=P),
                               allow_slow_non_contiguous=True).then_inc(small_loaded, 16)
            for n in range(2):
                pool.dma_start(bv_row[:, n, :], bv.rearrange("(a n) -> a n", a=1).broadcast_to([P, D]))\
                    .then_inc(small_loaded, 16)
            pool.dma_start(bo_row[:, :], bo.rearrange("(a n) -> a n", a=1).broadcast_to([P, D])).then_inc(small_loaded, 16)
            pool.dma_start(wo[:, :, :], Wo.rearrange("(t p) n -> p t n", p=P)).then_inc(small_loaded, 16)
            for n, v in enumerate((sbq, sbk, sbv)):
                pool.dma_start(sbv_col[:, n, :], v.rearrange("h d -> (h d)").rearrange("(t p) -> p t", p=P),
                               allow_slow_non_contiguous=True)\
                    .then_inc(small_loaded, 16)
            pool.dma_start(sbo_row[:, :], sbo.rearrange("(a n) -> a n", a=1).broadcast_to([P, D]))\
                .then_inc(small_loaded, 16)
            for n, v in enumerate((mu_r, mu_k)):
                pool.dma_start(mus[:, n, 0, :], v.rearrange("(t p) -> p t", p=P),
                               allow_slow_non_contiguous=True).then_inc(small_loaded, 16)
            pool.memset(ctxT_hi[:, :, LK:KPAD].bitcast(F32), 0.0).then_inc(pads_ready, 1)
            pool.memset(ctxT_lo[:, :, LK:KPAD].bitcast(F32), 0.0).then_inc(pads_ready, 1)
            pool.memset(mask_add[:, LK:KS], PADDED).then_inc(pads_ready, 1)

            def add_bias(j):
                pool.wait_ge(xn2_ready, j + 1)
                nc.gpsimd.tensor_tensor(xres[:, j, :], xres[:, j, :], sbo_row[:, :], ALU.add).then_inc(bias_added, 1)

            for j in range(EARLY):
                add_bias(j)
            pool.wait_ge(pv_free, 2 * B + 1)
            for j in range(TJ):
                wait_qk(pool, j)
                if j >= 2:
                    tring.wait_filled(pool, TUSE["S1", j - 2])
                for b2 in range(2):
                    nc.gpsimd.tensor_tensor(
                        k2_diag[:, (j % 2) * 4 + 2 + b2],
                        k2T[:, j, 1, b2 * LQ:(b2 + 1) * LQ].unsqueeze(1).broadcast_to([P, HH, LQ]),
                        head_mask.unsqueeze(2).broadcast_to([P, HH, LQ]), ALU.mult).then_inc(diag_ready[1], 1)
                if j == 1:
                    add_bias(TJ - 1)

        SMALL = 16 * 12
        PADS = 3

        @block.scalar
        def _(act):
            def copy(dst, src):
                return nc.scalar.activation(dst, src, ACT.Copy)

            def context_hi(n, u, b):
                tiles = min(2, KT - 2 * n)
                width = P * tiles if n < NC - 1 else KTAIL
                ring.wait_filled(act, u, b)
                src = ring.bank(u)[:, :].rearrange("p (t k) -> p t k", t=DH)[:, :, 0:width]
                copy(ctxT_hi[:, :, 2 * n * P:2 * n * P + width], src).then_inc(hi_ready, 1)

            def keys_hi(n, u, b, first=False):
                half, c = divmod(n, NCH)
                ring.wait_filled(act, u, b)
                if c == 0 and not first:
                    for g in range(4 * half, 4 * half + 4):
                        act.wait_ge(stacked[g], (b + 1) * 48)
                nc.scalar.activation(keysT[:, 0, half, c * CH:(c + 1) * CH].bitcast(F32R), ring.bank(u)[:, 0:CH],
                                     ACT.Identity, bias=cols[:, 1, half:half + 1]).then_inc(hi_ready, 1)

            def exps(b, g):
                s = b * G + g
                act.wait_ge(masked_ready, s + 1)
                nc.scalar.activation(probs[:, g % 2, 0:KS], probs[:, g % 2, 0:KS], ACT.Exp,
                                     bias=xmin[:, g % 2:g % 2 + 1], scale=-1.0,
                                     accum_out=psums[:, g:g + 1]).then_inc(probs_ready, 1)

            def take_qk(j, bank, freed):
                for n, dst in enumerate((q2T, k2T)):
                    for half in range(DH):
                        at = (n * DH + half) * P
                        last = nc.scalar.activation(dst[:, j, half], bank[:, at:at + P], ACT.Identity,
                                                    bias=sbv_col[:, n, half:half + 1])
                last.then_inc(freed, 1)

            for n in range(2):
                ring.wait_filled(act, FUSE["X", n])
                copy(xnT[:, n, :], ring.bank(FUSE["X", n])[:, :]).then_inc(ring.freed[FUSE["X", n] % 3], 1)
            act.wait_ge(small_loaded, SMALL)
            for n in range(NC):
                context_hi(n, FUSE["C", n], 0)
            for n in range(NK):
                keys_hi(n, FUSE["K", n], 0, first=True)
            exps(0, 0)

            def body(b, last):
                for g in range(G):
                    for f, tiles in enumerate(PT_TILES):
                        u = use(("PT", g, f), last)
                        ring.wait_filled(act, u, b)
                        bank = ring.bank(u)
                        done = copy(probsT[:, g % 4, tiles[0]:tiles[-1] + 1, :],
                                    bank[:, 0:len(tiles) * P].rearrange("p (t c) -> p t c", c=P))
                        if g % 4 == 3 and f == len(PT_TILES) - 1:
                            done = copy(recipT[:, :], bank[:, 3 * P:4 * P])
                        done.then_inc(ring.freed[u % 3], 1)
                    if g < G - 1:
                        exps(b, g + 1)
                    elif not last:
                        exps(b + 1, 0)
                    for kind, n in (SIDE_LAST if last else SIDE)[g]:
                        u = use((kind, n), last)
                        if kind == "C":
                            context_hi(n, u, b)
                        if kind == "W":
                            ring.wait_filled(act, u, b)
                            copy(wT(n)[:, :, :], ring.bank(u)[:, :].rearrange("p (t d) -> p t d", t=DH))\
                                .then_inc(ring.freed[u % 3], 1)
                        if kind == "K":
                            keys_hi(n, u, b)
                        if kind == "X":
                            ring.wait_filled(act, u, b)
                            nc.scalar.activation(xnT2[:, n].rearrange("p t c -> p (t c)"), ring.bank(u)[:, 0:D], ACT.Copy)\
                                .then_inc(ring.freed[u % 3], 1)
                        if kind == "QK":
                            ring.wait_filled(act, u, b)
                            take_qk(n, ring.bank(u), ring.freed[u % 3])

            with act.Fori(0, LAST) as b:
                body(b, False)
            body(LAST, True)

            act.wait_ge(pv_free, 2 * B + 1)
            for stage, j in TAIL:
                u = TUSE[stage, j]
                if stage in ("Y", "O", "Y2", "FV"):
                    continue
                tring.wait_filled(act, u)
                bank, freed = tring.bank(u), tring.freed[u % tring.n]
                if stage == "X":
                    copy(xnT2[:, j].rearrange("p t c -> p (t c)"), bank[:, 0:D]).then_inc(freed, 1)
                elif stage == "QK":
                    take_qk(j, bank, freed)
                elif stage == "V":
                    for h2 in range(2):
                        last = nc.scalar.activation(
                            v2[:, 2 * j:2 * j + 2, :, h2 * VW:h2 * VW + DK].rearrange("p b g d -> p (b g) d"),
                            bank[:, :].rearrange("p (a h d) -> p a h d", h=2, d=DK)[:, :, h2, :],
                            ACT.Identity, scale=pair_mask[:, h2 * DK:h2 * DK + 1])
                    last.then_inc(freed, 1)
                elif stage in ("S0", "S1"):
                    half = int(stage[1])
                    tring.wait_taken(act, [u])
                    rows = p2[:, (j % 2) * 2 + half]
                    nc.scalar.activation(rows, rows, ACT.Exp, scale=DK ** -0.5).then_inc(p2_ready[half], 1)
                elif stage in ("T0", "T1"):
                    if j >= 2:
                        tring.wait_filled(act, TUSE["O", j - 2])
                    copy(p2T[:, (j % 2) * 2 + int(stage[1])], bank[:, :].rearrange("p (g c) -> p g c", c=P))                        .then_inc(freed, 1)
                elif stage == "OT":
                    for half in range(DH):
                        last = nc.scalar.activation(attnT[:, half, j * P:(j + 1) * P], bank[:, half * P:(half + 1) * P],
                                                    ACT.Identity, bias=sbv_col[:, 2, half:half + 1])
                    last.then_inc(freed, 1)
                elif stage == "X3":
                    for n, dst in ((0, xrT), (1, xkT)):
                        for half in range(DH):
                            last = nc.scalar.activation(dst[:, j, half], bank[:, half * P:(half + 1) * P],
                                                        ACT.Copy, scale=mus[:, n, 0, half:half + 1])
                    last.then_inc(scaled_ready, 1)
                elif stage == "F":
                    keys = kaT[:, j].rearrange("p t c -> p (t c)")
                    nc.scalar.activation(keys, bank[:, 0:D], ACT.Relu).then_inc(relu_ready, 1)
                    nc.scalar.activation(gate[:, j], bank[:, D:2 * D], ACT.Tanh, scale=0.5).then_inc(freed, 1)
                    act.wait_ge(relu_ready, j + 1)
                    nc.scalar.activation(keys, keys, ACT.Square).then_inc(ka_ready, 1)

        @block.vector
        def _(dve):
            steps = [0]

            def link(ins):
                steps[0] += 1
                ins.then_inc(dve_step, 1)
                dve.wait_ge(dve_step, steps[0])

            def layernorm(tiles, dst, ready):
                j0, n = tiles[0], len(tiles)
                for j in tiles:
                    last = nc.vector.bn_stats(stats[:, j, :], xres[:, j, :])
                link(last)
                for j in tiles:
                    last = nc.vector.bn_aggr(mv[:, j, :], stats[:, j, :])
                link(last)
                v = [newton[:, i, 0:n] for i in range(3)]
                y, t, bits = newton[:, 3, 0:n], newton[:, 4, 0:n], newton_bits[:, 0, 0:n]
                link(nc.vector.tensor_scalar(v[0], mv[:, j0:j0 + n, 1], EPS, None, ALU.add))
                nc.vector.tensor_scalar(v[1], v[0], 0.25, None, ALU.mult)
                nc.vector.tensor_scalar(v[2], v[0], 0.0625, None, ALU.mult)
                link(nc.vector.tensor_scalar(bits, v[0].bitcast(I32), 1, None, ALU.logical_shift_right))
                link(nc.vector.tensor_scalar(y.bitcast(I32), bits, -1, RSQRT_SEED, ALU.mult, ALU.add))
                for i in range(3):
                    if n == 1:
                        link(nc.vector.scalar_tensor_tensor(out=t, in0=y, scalar=v[i], in1=y, op0=ALU.mult, op1=ALU.mult))
                    else:
                        link(nc.vector.tensor_tensor(t, y, y, ALU.mult))
                        link(nc.vector.tensor_tensor(t, t, v[i], ALU.mult))
                    link(nc.vector.scalar_tensor_tensor(out=y, in0=t, scalar=-3.0, in1=y, op0=ALU.add, op1=ALU.mult))
                link(nc.vector.tensor_scalar(rstd[:, j0:j0 + n], y, -0.125, None, ALU.mult))
                for j in tiles:
                    nc.vector.tensor_scalar(dst[:, j, :], xres[:, j, :], mv[:, j, 0:1], rstd[:, j:j + 1],
                                            ALU.subtract, ALU.mult).then_inc(ready, 1)

            def add_projection(j, bank, freed):
                nc.vector.tensor_tensor(xres[:, j, :], bank[:, 0:D], xres[:, j, :], ALU.add).then_inc(freed, 1)

            dve.wait_ge(x_loaded, 32)
            layernorm(range(TJ), xn, xn_ready)
            dve.wait_ge(w_loaded, 48)
            link(nc.vector.tensor_copy(wk_hi[:, :, :], w_raw[:, 1]))
            nc.vector.tensor_tensor(wk_lo[:, :, :], w_raw[:, 1], wk_hi[:, :, :], ALU.subtract).then_inc(weights_ready, 1)
            dve.wait_ge(small_loaded, SMALL)
            nc.vector.tensor_scalar(mus[:, :, 1, :], mus[:, :, 0, :], -1.0, 1.0, ALU.mult, ALU.add)
            for half in range(DH):
                u = FUSE["Q", half]
                ring.wait_filled(dve, u)
                nc.vector.tensor_scalar(qT[:, half, :], ring.bank(u)[:, :], cols[:, 0, half:half + 1], QSCALE,
                                        ALU.add, ALU.mult).then_inc(ring.freed[u % 3], 1)
            ring.wait_taken(dve, [FUSE["Q", half] for half in range(DH)])
            for h2 in range(2):
                for half in range(DH):
                    last = nc.vector.tensor_scalar(q_pair[:, half, :, h2, :],
                                                   qT[:, half, :].rearrange("p (b q) -> p b q", q=LQ),
                                                   side_mask[:, h2:h2 + 1], None, ALU.mult)
            link(last)
            flat = [v.rearrange("p a b c d -> p (a b c d)") for v in (q_pair, q_pair_hi, q_pair_lo)]
            nc.vector.tensor_copy(flat[1].bitcast(F32R), flat[0]).then_inc(q_pair_ready, 1)
            dve.wait_ge(q_pair_ready, 1)
            nc.vector.tensor_tensor(flat[2].bitcast(F32R), flat[0], flat[1], ALU.subtract).then_inc(q_pair_ready, 1)

            def make_mask(b):
                dve.wait_ge(mask_loaded, (b + 1) * 32)
                nc.vector.tensor_scalar(mask_add[:, 0:LK], mask_b[:, :], MASKED, None, ALU.mult).then_inc(mask_ready, 1)
                dve.wait_ge(mask_ready, b + 1)

            def context_lo(n, u, b, at):
                tiles = min(2, KT - 2 * n)
                width = P * tiles if n < NC - 1 else KTAIL
                dve.wait_ge(hi_ready, at)
                src = ring.bank(u)[:, :].rearrange("p (t k) -> p t k", t=DH)[:, :, 0:width]
                nc.vector.tensor_tensor(ctxT_lo[:, :, 2 * n * P:2 * n * P + width], src,
                                        ctxT_hi[:, :, 2 * n * P:2 * n * P + width], ALU.subtract)\
                    .then_inc(ring.freed[u % 3], 1)

            def keys_lo(n, u, b, at):
                half, c = divmod(n, NCH)
                dve.wait_ge(hi_ready, at)
                nc.vector.scalar_tensor_tensor(
                    out=keysT[:, 1, half, c * CH:(c + 1) * CH].bitcast(F32R), in0=ring.bank(u)[:, 0:CH],
                    scalar=cols[:, 1, half:half + 1], in1=keysT[:, 0, half, c * CH:(c + 1) * CH],
                    op0=ALU.add, op1=ALU.subtract).then_inc(ring.freed[u % 3], 1)

            def mask_scores(b, g):
                dve.wait_ge(scores_ready, b * G + g + 1)
                dve.nop(nofuse=True)
                nc.vector.tensor_tensor_reduce(
                    out=probs[:, g % 2, 0:KS].rearrange("p (n c) -> p n c", n=NCH),
                    in0=score_banks[:, :, 0:CH], in1=mask_add[:, :].rearrange("p (n c) -> p n c", n=NCH),
                    scale=1.0, scalar=3.0e38, op0=ALU.add, op1=ALU.min,
                    accum_out=xmin[:, g % 2:g % 2 + 1]).then_inc(masked_ready, 1)

            HI = NC + NK
            for n in range(NC):
                context_lo(n, FUSE["C", n], 0, n + 1)
            link(nc.vector.tensor_copy(wv_hi[:, :, :], w_raw[:, 2]))
            nc.vector.tensor_tensor(wv_lo[:, :, :], w_raw[:, 2], wv_hi[:, :, :], ALU.subtract).then_inc(weights_ready, 1)
            for n in range(NK):
                keys_lo(n, FUSE["K", n], 0, NC + n + 1)
            for j in range(TJ):
                last = nc.vector.tensor_tensor(xres[:, j, :], xres[:, j, :], bo_row[:, :], ALU.add)
            link(last)
            nc.vector.memset(probs[:, :, KS:KPAD], 0.0).then_inc(pv_free, 1)
            dve.wait_ge(pv_free, 1)
            dve.wait_ge(pads_ready, PADS)
            make_mask(0)
            mask_scores(0, 0)

            def body(b, last):
                made = 0
                for g in range(G):
                    if g < G - 1:
                        mask_scores(b, g + 1)
                    elif not last:
                        make_mask(b + 1)
                        mask_scores(b + 1, 0)
                    for kind, n in (SIDE_LAST if last else SIDE)[g]:
                        u = use((kind, n), last)
                        if kind == "V":
                            ring.wait_filled(dve, u, b)
                            tiles = min(2, KT - 2 * n)
                            nc.vector.tensor_tensor(
                                values[:, 2 * n:2 * n + tiles, :],
                                ring.bank(u)[:, 0:tiles * D].rearrange("p (t d) -> p t d", d=D),
                                bv_row[:, 0:tiles, :], ALU.add).then_inc(ring.freed[u % 3], 1)
                        elif kind in "CK":
                            made += 1
                            (context_lo if kind == "C" else keys_lo)(n, u, b, (b + 1) * HI + made)
                        elif kind == "Y":
                            if n == 0:
                                dve.wait_ge(tail_w_loaded, 16 * NW)
                            ring.wait_filled(dve, u, b)
                            add_projection(n, ring.bank(u), ring.freed[u % 3])
                            if n == EARLY - 1:
                                ring.wait_taken(dve, [use(("Y", j), last) for j in range(EARLY)], b)
                                layernorm(range(EARLY), xn2, xn2_ready)
                    if g % 4 == 2:
                        h = 2 * b + g // 4
                        dve.wait_ge(probs_ready, b * G + g + 2)
                        nc.vector.reciprocal(precip[:, :], psums[:, g - 2:g + 2]).then_inc(recip_step, 1)
                        dve.wait_ge(recip_step, h + 1)
                        nc.vector.tensor_tensor(
                            pair_recip[:, :, :], precip[:, :].unsqueeze(2).broadcast_to([P, 4, PAIR]),
                            pair_mask.unsqueeze(1).broadcast_to([P, 4, PAIR]), ALU.mult).then_inc(pair_recip_ready, 1)
                    if g % 4 == 3:
                        h = 2 * b + g // 4
                        dve.wait_ge(pv_ready, h + 1)
                        nc.vector.tensor_tensor(prod[:, :, :].rearrange("p h q -> p (h q)"), pv_bank[:, 0:P],
                                                recipT[:, :], ALU.mult).then_inc(prod_ready, 1)
                        dve.wait_ge(prod_ready, h + 1)
                        at = b * LQ
                        dst = attnT[:, g // 4, at:at + LQ] if type(b) is int else attnT[:, g // 4, bass.ds(at, LQ)]
                        nc.vector.tensor_tensor(dst, prod[:, 0, :], prod[:, 1, :], ALU.add).then_inc(pv_free, 1)

            with dve.Fori(0, LAST) as b:
                body(b, False)
            body(LAST, True)

            ones = v2.rearrange("p b g (h d) -> p (b g) h d", h=2)[:, :, :, DK]
            nc.vector.tensor_copy(ones, pair_mask.rearrange("p (h d) -> p h d", h=2)[:, :, 0].unsqueeze(1)
                                  .broadcast_to([P, TJ * 2 * G, 2])).then_inc(ones_ready, 1)
            for stage, j in TAIL:
                if stage in ("X", "QK", "T0", "T1", "OT", "F"):
                    continue
                u = TUSE[stage, j]
                if stage != "V":
                    tring.wait_filled(dve, u)
                bank, freed = tring.bank(u), tring.freed[u % tring.n]
                if stage == "Y":
                    add_projection(j, bank, freed)
                    tring.wait_taken(dve, [u])
                    layernorm([j], xn2, xn2_ready)
                elif stage == "V":
                    wait_qk(dve, j)
                    if j >= 2:
                        tring.wait_filled(dve, TUSE["S0", j - 2])
                    for b2 in range(2):
                        nc.vector.tensor_tensor(
                            k2_diag[:, (j % 2) * 4 + b2],
                            k2T[:, j, 0, b2 * LQ:(b2 + 1) * LQ].unsqueeze(1).broadcast_to([P, HH, LQ]),
                            head_mask.unsqueeze(2).broadcast_to([P, HH, LQ]), ALU.mult).then_inc(diag_ready[0], 1)
                elif stage in ("S0", "S1"):
                    half = int(stage[1])
                    s = bank[:, :].rearrange("p (h k) -> p h k", k=LQ)
                    link(nc.vector.tensor_reduce(max2[:, j, half, :], s, AX.X, ALU.max))
                    if j >= 2:
                        tring.wait_filled(dve, TUSE["T0" if half == 0 else "T1", j - 2])
                    nc.vector.tensor_tensor(p2[:, (j % 2) * 2 + half], s,
                                            max2[:, j, half, :].unsqueeze(2).broadcast_to([P, HH, LQ]),
                                            ALU.subtract).then_inc(freed, 1)
                elif stage == "O":
                    o = bank[:, 0:G * 2 * VW].rearrange("p (h d) -> p h d", d=VW)
                    link(nc.vector.reciprocal(recip2[:, j, :], o[:, :, DK]))
                    nc.vector.tensor_tensor(o2[:, j].rearrange("p (h d) -> p h d", d=DK), o[:, :, 0:DK],
                                            recip2[:, j, :].unsqueeze(2).broadcast_to([P, H, DK]), ALU.mult).then_inc(freed, 1)
                elif stage == "Y2":
                    dve.wait_ge(bias_added, j + 1)
                    add_projection(j, bank, freed)
                    tring.wait_taken(dve, [u])
                    layernorm([j], xn2, xn3_ready)
                elif stage == "X3":
                    dve.wait_ge(scaled_ready, j + 1)
                    for n, dst in ((0, xrT), (1, xkT)):
                        for half in range(DH):
                            mixed = dst[:, j, half].rearrange("p (b q) -> p b q", q=LQ)[:, :, 1:LQ]
                            before = bank[:, half * P:(half + 1) * P].rearrange("p (b q) -> p b q", q=LQ)[:, :, 0:LQ - 1]
                            last = nc.vector.scalar_tensor_tensor(
                                out=mixed, in0=before, scalar=mus[:, n, 1, half:half + 1], in1=mixed,
                                op0=ALU.mult, op1=ALU.add)
                    last.then_inc(freed, 1)
                elif stage == "FV":
                    tring.wait_taken(dve, [TUSE["F", j]])
                    nc.vector.scalar_tensor_tensor(out=gate[:, j], in0=gate[:, j], scalar=1.0, in1=bank[:, 0:D],
                                                   op0=ALU.add, op1=ALU.mult).then_inc(freed, 1)
                    tring.wait_taken(dve, [u])
                    nc.vector.scalar_tensor_tensor(out=xres[:, j, :], in0=gate[:, j], scalar=0.5, in1=xres[:, j, :],
                                                   op0=ALU.mult, op1=ALU.add).then_inc(sum_ready, 1)

        @block.tensor
        def _(pe):
            def transposes(dst, srcs):
                for n, src in enumerate(srcs):
                    rows, width = src.shape[0], src.shape[1]
                    last = nc.tensor.transpose(dst[0:width, n * P:n * P + rows], src, ident[0:rows, 0:rows])
                return last

            def accumulate(dst, terms):
                for n, (a, c) in enumerate(terms):
                    last = nc.tensor.matmul(dst, a, c, start=(n == 0), stop=(n == len(terms) - 1))
                return last

            def three_passes(dst, terms):
                terms = [t for ah, al, bh, bl in terms for t in ((ah, bh), (al, bh), (ah, bl))]
                for n, (a, c) in enumerate(terms):
                    last = nc.tensor.matmul(dst, a, c, start=(n == 0), stop=(n == len(terms) - 1))
                return last

            def context_transposes(n, u, b, wait):
                ring.wait_free(pe, u, b)
                if n == 0:
                    pe.wait_ge(context_loaded, wait)
                bank = ring.bank(u)
                for half in range(DH):
                    for t in range(2 * n, min(2 * n + 2, KT)):
                        rows = P if t < KT - 1 else KTAIL
                        at = half * 2 * P + (t - 2 * n) * P
                        last = nc.tensor.transpose(bank[:, at:at + rows],
                                                   context[0:rows, t, half * P:(half + 1) * P], ident[0:rows, 0:rows])
                last.then_inc(ring.filled[u % 3], 1)

            def project_keys(n, u, b, first):
                half, c = divmod(n, NCH)
                ring.wait_free(pe, u, b)
                cs = slice(half * P, (half + 1) * P)
                ks = slice(c * CH, (c + 1) * CH)
                three_passes(ring.bank(u)[:, 0:CH],
                             [(wk_hi[:, t, cs], wk_lo[:, t, cs], ctxT_hi[:, t, ks], ctxT_lo[:, t, ks])
                              for t in range(DH)]).then_inc(ring.filled[u % 3], 1)

            def project_values(n, u, b):
                ring.wait_free(pe, u, b)
                for i, t in enumerate(range(2 * n, min(2 * n + 2, KT))):
                    ks = slice(t * P, (t + 1) * P)
                    last = three_passes(ring.bank(u)[:, i * D:(i + 1) * D],
                                        [(ctxT_hi[:, d, ks], ctxT_lo[:, d, ks], wv_hi[:, d, :], wv_lo[:, d, :])
                                         for d in range(DH)])
                last.then_inc(ring.filled[u % 3], 1)

            def project_output(j, bank, w):
                return accumulate(bank[:, 0:D], [(attnT[:, t, j * P:(j + 1) * P], w[:, t, :]) for t in range(DH)])

            def transpose_tokens(j, bank):
                return transposes(bank, [xn2[:, j, half * P:(half + 1) * P] for half in range(DH)])

            def project_qk(j, bank):
                for n, w in enumerate((W_Q, W_K)):
                    for half in range(DH):
                        at = (n * DH + half) * P
                        last = accumulate(bank[:, at:at + P], [(wT(w)[:, t, half * P:(half + 1) * P], xnT2[:, j, t])
                                                               for t in range(DH)])
                return last

            def scores(b, g):
                if type(b) is not int or b * G + g > 0:
                    pe.wait_ge(masked_ready, b * G + g)
                if g % 4 == 0:
                    pe.wait_ge(q_second_loaded if g else q_first_loaded, (b + 1) * 16)
                pe.wait_ge(stacked[g], (b + 1) * 48)
                for c in range(NCH):
                    last = nc.tensor.matmul(score_banks[:, c, 0:CH], q_stack[:, g, :],
                                            k_stack[:, g, c * CH:(c + 1) * CH], start=True, stop=True)
                last.then_inc(scores_ready, 1)

            for half in range(DH):
                u = FUSE["X", half]
                pe.wait_ge(xn_ready, TJ)
                transposes(ring.bank(u), [xn[:, j, half * P:(half + 1) * P] for j in range(TJ)])\
                    .then_inc(ring.filled[u % 3], 1)
            ring.wait_taken(pe, [FUSE["X", half] for half in range(DH)])
            pe.wait_ge(w_loaded, 48)
            for half in range(DH):
                u = FUSE["Q", half]
                ring.wait_free(pe, u)
                for t in range(DH):
                    last = nc.tensor.matmul(ring.bank(u)[:, :], w_raw[:, 0, t, half * P:(half + 1) * P],
                                            xnT[:, t, :], start=(t == 0), stop=(t == DH - 1))
                last.then_inc(ring.filled[u % 3], 1)
            for n in range(NC):
                context_transposes(n, FUSE["C", n], 0, 32)
            pe.wait_ge(weights_ready, 1)
            pe.wait_ge(pads_ready, PADS)
            ring.wait_taken(pe, [FUSE["C", n] for n in range(NC)])
            for n in range(NK):
                project_keys(n, FUSE["K", n], 0, True)
            scores(0, 0)
            pe.wait_ge(weights_ready, 2)

            def body(b, last_batch):
                for g in range(G):
                    if g < G - 1:
                        scores(b, g + 1)
                    elif not last_batch:
                        scores(b + 1, 0)
                    pe.wait_ge(probs_ready, b * G + g + 1)
                    for f, tiles in enumerate(PT_TILES):
                        u = use(("PT", g, f), last_batch)
                        ring.wait_free(pe, u, b)
                        srcs = [probs[:, g % 2, t * P:(t + 1) * P] for t in tiles]
                        if g % 4 == 3 and f == len(PT_TILES) - 1:
                            pe.wait_ge(pair_recip_ready, 2 * b + g // 4 + 1)
                            srcs.append(pair_recip[:, :, :].rearrange("p a b -> p (a b)"))
                        transposes(ring.bank(u), srcs).then_inc(ring.filled[u % 3], 1)
                    for kind, n in (SIDE_LAST if last_batch else SIDE)[g]:
                        u = use((kind, n), last_batch)
                        if kind == "V":
                            project_values(n, u, b)
                        elif kind == "C":
                            context_transposes(n, u, b, (b + 2) * 32)
                        elif kind == "W":
                            ring.wait_free(pe, u, b)
                            if n == 0:
                                pe.wait_ge(tail_w_loaded, 16 * NW)
                            for half in range(DH):
                                for t in range(DH):
                                    at = half * D + t * P
                                    last = nc.tensor.transpose(ring.bank(u)[:, at:at + P],
                                                               w_nat[:, n, t, half * P:(half + 1) * P], ident)
                            last.then_inc(ring.filled[u % 3], 1)
                        elif kind == "Y":
                            ring.wait_free(pe, u, b)
                            project_output(n, ring.bank(u), wo).then_inc(ring.filled[u % 3], 1)
                        elif kind == "X":
                            ring.wait_free(pe, u, b)
                            pe.wait_ge(xn2_ready, n + 1)
                            transpose_tokens(n, ring.bank(u)).then_inc(ring.filled[u % 3], 1)
                        elif kind == "QK":
                            ring.wait_taken(pe, [use((k, m), True) for k, m in (("X", n), ("W", NW - 1))], b)
                            ring.wait_free(pe, u, b)
                            project_qk(n, ring.bank(u)).then_inc(ring.filled[u % 3], 1)
                        else:
                            if n == 0:
                                ring.wait_taken(pe, [use(("C", m)) for m in range(NC)], b)
                            project_keys(n, u, b, False)
                    if g % 4 == 3:
                        need = [use(("PT", i, f), last_batch) for i in range(g - 3, g + 1) for f in range(len(PT_TILES))]
                        if g == 3:
                            need = [use(("V", n), last_batch) for n in range(NV)] + need
                        pe.wait_ge(pv_free, 2 * b + g // 4 + 1)
                        ring.wait_taken(pe, need, b)
                        for t in range(KT):
                            for p in range(4):
                                ch = (g - 3 + p) * PAIR
                                last = nc.tensor.matmul(pv_bank[p * PAIR:(p + 1) * PAIR, 0:P],
                                                        values[:, t, ch:ch + PAIR], probsT[:, p, t, :],
                                                        start=(t == 0), stop=(t == KT - 1))
                        last.then_inc(pv_ready, 1)

            with pe.Fori(0, LAST) as b:
                body(b, False)
            body(LAST, True)

            ring.wait_taken(pe, [use(("PT", G - 1, f), True) for f in range(len(PT_TILES))] + [use(("QK", EARLY - 1), True)], LAST)
            pe.wait_ge(masked_ready, B * G)
            pe.wait_ge(pv_free, 2 * B + 1)
            for stage, j in TAIL:
                u = TUSE[stage, j]
                tring.wait_free(pe, u)
                bank = tring.bank(u)
                if stage == "Y":
                    last = project_output(j, bank, wo)
                elif stage == "X":
                    pe.wait_ge(xn2_ready, j + 1)
                    last = transpose_tokens(j, bank)
                elif stage == "QK":
                    tring.wait_taken(pe, [TUSE["X", j]])
                    last = project_qk(j, bank)
                elif stage == "V":
                    for b2 in range(2):
                        for t in range(DH):
                            for h2 in range(2):
                                last = nc.tensor.matmul(bank[h2 * LQ:(h2 + 1) * LQ, b2 * D:(b2 + 1) * D],
                                                        xnT2[:, j, t, b2 * LQ:(b2 + 1) * LQ], wT(W_V)[:, t, :],
                                                        start=(t == 0), stop=(t == DH - 1), skip_group_check=True)
                elif stage in ("S0", "S1"):
                    half = int(stage[1])
                    wait_qk(pe, j)
                    pe.wait_ge(diag_ready[half], 2 * j + 2)
                    for b2 in range(2):
                        last = nc.tensor.matmul(bank[b2 * LQ:(b2 + 1) * LQ, :], q2T[:, j, half, b2 * LQ:(b2 + 1) * LQ],
                                                k2_diag[:, (j % 2) * 4 + half * 2 + b2].rearrange("p h k -> p (h k)"),
                                                start=True, stop=True)
                elif stage in ("T0", "T1"):
                    half = int(stage[1])
                    pe.wait_ge(p2_ready[half], j + 1)
                    flat = p2[:, (j % 2) * 2 + half].rearrange("p h k -> p (h k)")
                    last = transposes(bank, [flat[:, i * P:(i + 1) * P] for i in range(4)])
                elif stage == "O":
                    tring.wait_taken(pe, [TUSE[s, j] for s in ("V", "T0", "T1")])
                    if j == 0:
                        pe.wait_ge(ones_ready, 1)
                    for g in range(G):
                        for b2 in range(2):
                            last = nc.tensor.matmul(bank[b2 * LQ:(b2 + 1) * LQ, g * 2 * VW:(g + 1) * 2 * VW],
                                                    p2T[:, (j % 2) * 2 + g // 4, g % 4, b2 * LQ:(b2 + 1) * LQ],
                                                    v2[:, 2 * j + b2, g, :], start=True, stop=True, skip_group_check=True)
                elif stage == "OT":
                    tring.wait_taken(pe, [TUSE["O", j]])
                    last = transposes(bank, [o2[:, j, half * P:(half + 1) * P] for half in range(DH)])
                elif stage == "Y2":
                    tring.wait_taken(pe, [TUSE["OT", j]])
                    last = project_output(j, bank, wT(W_O))
                elif stage == "X3":
                    pe.wait_ge(xn3_ready, j + 1)
                    last = transpose_tokens(j, bank)
                elif stage == "F":
                    tring.wait_taken(pe, [TUSE["X3", j]])
                    for half in range(DH):
                        accumulate(bank[:, half * P:(half + 1) * P],
                                   [(wT(W_FK)[:, t, half * P:(half + 1) * P], xkT[:, j, t]) for t in range(DH)])
                    last = accumulate(bank[:, D:2 * D], [(xrT[:, j, t], wT(W_FR)[:, t, :]) for t in range(DH)])
                else:
                    pe.wait_ge(ka_ready, j + 1)
                    last = accumulate(bank[:, 0:D], [(kaT[:, j, t], wT(W_FV)[:, t, :]) for t in range(DH)])
                last.then_inc(tring.filled[u % tring.n], 1)


_INS = ["x", "ctx_1024", "mask_BxSxS2_bf0",
        "L0_xattn_Wq", "L0_xattn_bq", "L0_xattn_Wk", "L0_xattn_bk", "L0_xattn_Wv", "L0_xattn_bv",
        "L0_xattn_Wo", "L0_xattn_bo",
        "L0_attn_Wq", "L0_attn_bq", "L0_attn_Wk", "L0_attn_bk", "L0_attn_Wv", "L0_attn_bv",
        "L0_attn_Wo", "L0_attn_bo",
        "L0_ffn_W_r", "L0_ffn_W_k", "L0_ffn_W_v", "L0_ffn_mu_r", "L0_ffn_mu_k"]


def shape_constants(np):
    c = np.zeros((P, CONSTS), np.float32)
    row = np.arange(P)
    c[:, C_ID:C_ID + P] = np.eye(P, dtype=np.float32)
    c[:, C_PAIR:C_PAIR + 32] = (row[:, None] // 64) == (np.arange(32)[None, :] // 16)
    c[:, C_HEAD:C_HEAD + 8] = (row[:, None] // 16) == np.arange(8)[None, :]
    c[:, C_SIDE:C_SIDE + 2] = (row[:, None] // 16) % 2 == np.arange(2)[None, :]
    return c


def kernel(**inputs):
    import numpy as _np
    import concourse.bacc as _bacc
    from concourse import mybir as _mybir
    from concourse.bass_utils import run_bass_kernel_spmd as _run

    nc = _bacc.Bacc("TRN2", target_bir_lowering=False, num_devices=1)
    arrays, args = {}, []
    for name in _INS:
        a = _np.ascontiguousarray(inputs[name])
        arrays[f"in_{name}_dram"] = a
        args.append(nc.dram_tensor(f"in_{name}_dram", a.shape, _mybir.dt.from_np(a.dtype), kind="ExternalInput").ap())
    a = shape_constants(_np)
    arrays["in_consts_dram"] = a
    args.append(nc.dram_tensor("in_consts_dram", a.shape, _mybir.dt.from_np(a.dtype), kind="ExternalInput").ap())
    args.append(nc.dram_tensor("out_0_dram", (8, 64, 256), _mybir.dt.float32, kind="ExternalOutput").ap())
    perceiver_layer(nc, *args)
    r = _run(nc, [arrays], core_ids=[0])
    return r.results[0]["out_0_dram"]
```

```python
import concourse.bass as bass
from concourse import mybir
from contextlib import ExitStack

F32 = mybir.dt.float32
F32R = mybir.dt.float32r
BF16 = mybir.dt.bfloat16
I32 = mybir.dt.int32
U8 = mybir.dt.uint8
ALU = mybir.AluOpType
ACT = mybir.ActivationFunctionType
AX = mybir.AxisListType

P = 128

C_ID, C_PAIR, C_HEAD, C_SIDE = 0, 128, 160, 168
CONSTS = 176


class Ring:

    def __init__(self, banks, filled, freed, per_batch=0):
        self.banks, self.filled, self.freed = banks, filled, freed
        self.n, self.turns = len(banks), per_batch // len(banks)

    def bank(self, u):
        return self.banks[u % self.n]

    def count(self, u, batch):
        return batch * self.turns + u // self.n if self.turns else u // self.n

    def wait_free(self, eng, u, batch=0):
        if u >= self.n:
            eng.wait_ge(self.freed[u % self.n], self.count(u, batch))

    def wait_filled(self, eng, u, batch=0):
        eng.wait_ge(self.filled[u % self.n], self.count(u, batch) + 1)

    def last_fills(self, us):
        last = {}
        for u in us:
            last[u % self.n] = u
        return [(n, u // self.n + 1) for n, u in last.items()]

    def wait_taken(self, eng, us, batch=0):
        for n, count in self.last_fills(us):
            eng.wait_ge(self.freed[n], batch * self.turns + count if self.turns else count)


def perceiver_layer(
    nc, x, ctx, mask, Wq, bq, Wk, bk, Wv, bv, Wo, bo,
    sWq, sbq, sWk, sbk, sWv, sbv, sWo, sbo, fWr, fWk, fWv, mu_r, mu_k, consts, out,
):
    B, LQ, D = x.shape
    LK = ctx.shape[1]
    H = 16
    DK = D // H
    DH = D // P
    G = H // 2
    PAIR = 2 * DK
    KT = -(-LK // P)
    KTAIL = LK - (KT - 1) * P
    KPAD = KT * P
    CH = 402
    NCH = 4
    KS = NCH * CH
    T = B * LQ
    TJ = T // P
    LAST = B - 1
    QSCALE = -1.0 / DK ** 0.5
    MASKED = 2.0 ** 60
    PADDED = 2.0 ** 100
    EPS = 1e-5
    RSQRT_SEED = 0x5F3759DF
    assert T % P == 0 and KS >= LK and CH % 2 == 0 and 2 * LQ == P

    PT_TILES = [range(0, 2), range(2, 6), range(6, 10), range(10, 13)]
    LAST_PT = len(PT_TILES) - 1
    NV = NC = (KT + 1) // 2
    NK = DH * NCH
    NW = 7

    def turns_of(*turns):
        return [[(item.rstrip("0123456789"), int(item.lstrip("PVCKWYXQ"))) for item in turn.split()] for turn in turns]

    WORK = turns_of(
        "P0 P1 P2 V0 P3 V1 V2",
        "P0 P1 P2 P3 V3 V4 C0 C1",
        "P0 P1 P2 P3 V5 V6 C2 C3",
        "P0 P1 P2 P3 C4 C5 C6",
        "P0 P1 P2 P3 K0 K1 K2",
        "P0 P1 P2 P3 K3 K4 K5",
        "P0 P1 P2 P3 K6",
        "P0 P1 P2 P3 K7",
    )
    WORK_LAST = turns_of(
        "P0 P1 P2 P3 V0 V1 V2",
        "P0 P1 P2 P3 V3 V4",
        "V5 P0 P1 P2 P3 V6 W0",
        "P0 P1 P2 P3 W1 Y0 Y1 Y2 W2 W3 W4",
        "P0 P1 P2 P3 W5",
        "P0 P1 P2 P3 W6 X0 X1",
        "P0 P1 P2 P3 X2 QK0 QK1",
        "P0 P1 P2 P3 QK2",
    )
    EARLY = TJ - 1

    def uses(work):
        order = [("P", g, n) if kind == "P" else (kind, n) for g in range(G) for kind, n in work[g]]
        return {item: n for n, item in enumerate(order)}

    USE, USE_LAST = uses(WORK), uses(WORK_LAST)
    PER = len(USE)
    PIECES = [range(0, 4), range(4, 8), range(8, 12), range(12, KT)]
    XQ = {item: n for n, item in enumerate([("X", 0), ("X", 1), ("Q", 0), ("Q", 1)])}
    FIRST = [("C", n) for n in range(NC)] + [("K", n) for n in range(NK)]
    FUSE = {item: n for n, item in enumerate(FIRST)}
    BASE = len(FIRST)

    STAGES = ["Y", "X", "QK", "V", "S0", "S1", "T0", "T1", "O", "OT", "Y2", "X3", "F", "FV"]
    SKEW = [0, 1, 2, 3]
    LATE_SKEW = [2, 2, 2, 3]
    NORM_TILES = [range(0, 3), range(3, 4)]
    TAIL = sorted(((n, j) for n in range(len(STAGES)) for j in range(TJ) if j >= EARLY or n >= 3),
                  key=lambda nj: (nj[0] + (SKEW if nj[0] < STAGES.index("X3") else LATE_SKEW)[nj[1]], nj[1]))
    TAIL = [(STAGES[n], j) for n, j in TAIL]
    TUSE = {item: n for n, item in enumerate(TAIL)}

    with ExitStack() as stack:
        def sb(name, shape, dt):
            return stack.enter_context(nc.sbuf_tensor(name, shape, dt))

        def sem(name):
            return stack.enter_context(nc.semaphore(name))

        context = sb("context", [P, KT, D], F32)
        ctxT_hi = sb("ctxT_hi", [P, DH, KPAD], F32R)
        ctxT_lo = sb("ctxT_lo", [P, DH, KPAD], F32R)
        keysT = sb("keysT", [P, 2, DH, KS], F32)
        k_stack = sb("k_stack", [3 * PAIR, G, KS], F32R)
        q_stack = sb("q_stack", [3 * PAIR, G, P], F32R)
        probs = sb("probs", [P, 2, KPAD], F32)
        probsT = sb("probsT", [P, 4, KT, P], F32)
        values = sb("values", [P, KT, D], F32)
        mask_b = sb("mask_b", [P, LK], U8)
        mask_add = sb("mask_add", [P, KS], BF16)
        wk_hi = sb("wk_hi", [P, DH, D], F32R)
        wk_lo = sb("wk_lo", [P, DH, D], F32R)
        wv_hi = sb("wv_hi", [P, DH, D], F32R)
        wv_lo = sb("wv_lo", [P, DH, D], F32R)
        wo = sb("wo", [P, DH, D], F32)
        attnT = sb("attnT", [P, DH, T], F32)
        xres = sb("xres", [P, TJ, D], F32)
        cst = sb("cst", [P, CONSTS], F32)
        cols = sb("cols", [P, 2, DH], F32)
        q_scale = sb("q_scale", [P, 2], F32)
        q_bias = sb("q_bias", [P, DH, 2], F32)
        bv_row = sb("bv_row", [P, 2, D], F32)
        bo_row = sb("bo_row", [P, D], F32)
        xmin = sb("xmin", [P, 2], F32)
        psums = sb("psums", [P, G], F32)
        precip = sb("precip", [P, 4], F32)
        pair_recip = sb("pair_recip", [P, 4, PAIR], F32)
        recipT = sb("recipT", [P, P], F32)
        prod = sb("prod", [P, 2, LQ], F32)
        stats = sb("stats", [P, TJ, 6], F32)
        mv = sb("mv", [P, TJ, 2], F32)
        rstd = sb("rstd", [P, TJ], F32)
        newton = sb("newton", [P, 5, TJ], F32)
        newton_bits = sb("newton_bits", [P, 1, TJ], I32)
        sbv_col = sb("sbv_col", [P, 3, DH], F32)
        sbo_row = sb("sbo_row", [P, D], F32)
        mus = sb("mus", [P, 2, 2, DH], F32)

        ident = cst[:, C_ID:C_ID + P]
        pair_mask = cst[:, C_PAIR:C_PAIR + PAIR]
        head_mask = cst[:, C_HEAD:C_HEAD + H // DH]
        side_mask = cst[:, C_SIDE:C_SIDE + 2]

        flat_pT = probsT[:, :, :, :].rearrange("p a b c -> p (a b c)")
        flat_p = probs[:, :, :].rearrange("p a b -> p (a b)")
        flat_v = values[:, :, :].rearrange("p a b -> p (a b)")
        flat_c = context[:, :, :].rearrange("p a b -> p (a b)")
        flat_k = keysT[:, :, :, :].rearrange("p a b c -> p (a b c)")

        def part(flat, at, *shape):
            size = 1
            for s in shape:
                size *= s
            v = flat[:, at:at + size]
            if len(shape) == 2:
                return v.rearrange("p (a b) -> p a b", b=shape[1])
            if len(shape) == 3:
                return v.rearrange("p (a b c) -> p a b c", b=shape[1], c=shape[2])
            return v.rearrange("p (a b c d) -> p a b c d", b=shape[1], c=shape[2], d=shape[3])

        xn = part(flat_p, 0, TJ, D)
        xnT = part(flat_p, TJ * D, DH, T)
        w_raw = part(flat_v, 0, 3, DH, D)
        q_pair = part(flat_pT, 2560, DH, B, 2, LQ)
        q_pair_hi = part(flat_c, 0, DH, B, 2, LQ)
        q_pair_lo = part(flat_pT, 4608, DH, B, 2, LQ)
        Q_LO_TILE = 4608 // (KT * P)

        score_banks = stack.enter_context(nc.psum_tensor("score_banks", [P, NCH, 512], F32))
        ring_banks = [stack.enter_context(nc.psum_tensor(f"ring{n}", [P, 512], F32)) for n in range(3)]
        pv_bank = stack.enter_context(nc.psum_tensor("pv_bank", [P, 512], F32))

        q_dram = nc.dram_tensor("q_pairs", (2, B, DH, P, P), F32, kind="Internal").ap()

        x_loaded = sem("x_loaded")
        w_loaded = [sem(f"w_loaded{n}") for n in range(3)]
        piece_loaded = [sem(f"piece_loaded{n}") for n in range(len(PIECES))]
        bias_loaded = sem("bias_loaded")
        small_loaded = sem("small_loaded")
        context_loaded = sem("context_loaded")
        mask_loaded = sem("mask_loaded")
        q_hi_stored = sem("q_hi_stored")
        q_lo_stored = sem("q_lo_stored")
        q0_stored = sem("q0_stored")
        q_first_loaded = sem("q_first_loaded")
        q_second_loaded = sem("q_second_loaded")
        stacked = [sem(f"stacked{g}") for g in range(G)]
        tail_w_loaded = sem("tail_w_loaded")
        out_stored = sem("out_stored")

        dve_step = sem("dve_step")
        pads_ready = sem("pads_ready")
        xn_ready = sem("xn_ready")
        q_scale_ready = sem("q_scale_ready")
        q_hi_ready = sem("q_hi_ready")
        q_lo_ready = sem("q_lo_ready")
        bo_added = sem("bo_added")
        w_hi_ready = sem("w_hi_ready")
        wk_ready = sem("wk_ready")
        wv_ready = sem("wv_ready")
        hi_ready = sem("hi_ready")
        mask_ready = sem("mask_ready")
        scores_ready = sem("scores_ready")
        masked_ready = sem("masked_ready")
        probs_ready = sem("probs_ready")
        recip_step = sem("recip_step")
        pair_recip_ready = sem("pair_recip_ready")
        pv_ready = sem("pv_ready")
        prod_ready = sem("prod_ready")
        pv_free = sem("pv_free")
        ring = Ring(ring_banks, [sem(f"filled{n}") for n in range(3)], [sem(f"freed{n}") for n in range(3)], PER)
        xq = Ring([score_banks[:, n, :] for n in range(NCH)], [sem(f"xq_filled{n}") for n in range(4)], [sem(f"xq_freed{n}") for n in range(4)])
        tail_banks = [score_banks[:, n, :] for n in range(NCH)] + [r[:, :] for r in ring_banks] + [pv_bank[:, :]]
        tring = Ring(tail_banks, [sem(f"tfilled{n}") for n in range(8)], [sem(f"tfreed{n}") for n in range(8)])
        assert PER % 3 == 0

        def use(item, last=False):
            return BASE + (USE_LAST if last else USE)[item]

        w_nat = part(flat_k, 0, NW, DH, D)
        wT6 = part(flat_c, 0, 6, DH, D)
        wT1 = sb("wT1", [P, DH, D], F32)

        def wT(n):
            return wT6[:, n] if n < 6 else wT1

        W_Q, W_K, W_V, W_O, W_FR, W_FK, W_FV = range(NW)

        HH = H // DH
        VW = DK + 1
        at_k = NW * DH * D
        xn2 = part(flat_k, at_k, TJ, D)
        xnT2 = part(flat_k, at_k + TJ * D, TJ, DH, P)
        q2T = part(flat_k, 0, TJ, DH, P)
        k2T = part(flat_k, TJ * D, TJ, DH, P)
        xrT = part(flat_k, 2 * TJ * D, TJ, DH, P)
        xkT = part(flat_p, TJ * 2 * D, TJ, DH, P)
        k2_diag = part(flat_pT, 0, 2 * DH * 2, HH, LQ)
        p2T = part(flat_pT, 2 * DH * 2 * HH * LQ, 2 * DH, 4, P)
        p2 = part(flat_p, 0, 2 * DH, HH, LQ)
        v2 = part(flat_v, 0, TJ * 2, G, 2 * VW)
        o2 = part(flat_v, TJ * 2 * G * 2 * VW, TJ, D)
        kaT, gate = xnT2, xn2
        xn2_ready = sem("xn2_ready")
        diag_ready = [sem("diag_ready0"), sem("diag_ready1")]
        ones_ready = sem("ones_ready")
        bias_added = sem("bias_added")
        p2_ready = [sem("p2_ready0"), sem("p2_ready1")]
        xn3_ready = sem("xn3_ready")
        scaled_ready = sem("scaled_ready")
        relu_ready = sem("relu_ready")
        ka_ready = sem("ka_ready")
        sum_ready = sem("sum_ready")

        def wait_qk(eng, j):
            if j < EARLY:
                ring.wait_taken(eng, [use(("QK", j), True)], LAST)
            else:
                tring.wait_taken(eng, [TUSE["QK", j]])

        max2 = sb("max2", [P, TJ, DH, HH], F32)
        recip2 = sb("recip2", [P, TJ, H], F32)

        def load_context(eng, b):
            src = ctx[b] if type(b) is int else \
                ctx.rearrange("b s d -> (b s d)")[bass.ds(b, LK * D)].rearrange("(s d) -> s d", d=D)
            eng.dma_start(context[:, 0:KT - 1, :],
                          src[0:(KT - 1) * P, :].rearrange("(t p) d -> p t d", p=P)).then_inc(context_loaded, 16)
            eng.dma_start(context[0:KTAIL, KT - 1, :], src[(KT - 1) * P:LK, :]).then_inc(context_loaded, 16)

        def stackings(g, b):
            return (b + 1) * 48 + (48 if g == 1 else 0)

        SMALL = 16 * 10
        PADS = 3
        block = stack.enter_context(nc.Block())

        @block.sync
        def _(sp):
            sp.dma_start(xres[:, :, :], x.rearrange("(j b) q d -> (b q) j d", b=2)).then_inc(x_loaded, 16)
            sp.dma_start(cst[:, :], consts).then_inc(x_loaded, 16)

            def load_mask(b):
                for h2 in range(2):
                    src = mask[b] if type(b) is int else \
                        mask.rearrange("b q s -> (b q s)")[bass.ds(b, LQ * LK)].rearrange("(q s) -> q s", s=LK)
                    sp.dma_start(mask_b[h2 * LQ:(h2 + 1) * LQ, :], src).then_inc(mask_loaded, 16)

            def load_q(b, second, pairs=range(4), loaded=None):
                for n, which in enumerate((0, 1, 0)):
                    src = q_dram[which, b, second] if type(b) is int else \
                        q_dram.rearrange("w b h r c -> (w b h r c)")[bass.ds(b + (which * B * DH + second) * P * P, P * P)]\
                        .rearrange("(r c) -> r c", c=P)
                    g = second * 4 + pairs[0]
                    sp.dma_start(q_stack[n * PAIR:(n + 1) * PAIR, g:g + len(pairs), :].bitcast(F32),
                                 src.rearrange("(p r) c -> r p c", p=4)[:, pairs[0]:pairs[-1] + 1])\
                      .then_inc(loaded or (q_second_loaded if second else q_first_loaded), 16)

            def stack_keys(half, pairs=range(4)):
                for p in pairs:
                    g = 4 * half + p
                    for n, which in enumerate((0, 0, 1)):
                        sp.dma_start(k_stack[n * PAIR:(n + 1) * PAIR, g, :].bitcast(F32),
                                     keysT[p * PAIR:(p + 1) * PAIR, which, half, :])\
                          .then_inc(stacked[g], 16)

            def load_piece(n):
                tiles = PIECES[n]
                full = min(tiles[-1] + 1, KT - 1)
                if full > tiles[0]:
                    sp.dma_start(context[:, tiles[0]:full, :],
                                 ctx[0, tiles[0] * P:full * P, :].rearrange("(t p) d -> p t d", p=P)).then_inc(piece_loaded[n], 16)
                if full <= tiles[-1]:
                    sp.dma_start(context[0:KTAIL, KT - 1, :], ctx[0, (KT - 1) * P:LK, :]).then_inc(piece_loaded[n], 16)

            def load_w(n, w):
                sp.dma_start(w_raw[:, n], w.rearrange("(t p) n -> p t n", p=P)).then_inc(w_loaded[n], 16)

            for n in range(2):
                load_piece(n)
            load_w(1, Wk)
            load_w(0, Wq)
            for n in range(2, len(PIECES)):
                load_piece(n)
            load_w(2, Wv)
            load_mask(0)
            sp.wait_ge(q_hi_ready, 1)
            sp.wait_ge(q_lo_ready, 1)
            for n, src in enumerate((q_pair_hi, q_pair_lo, q_pair_hi)):
                sp.dma_start(q_stack[n * PAIR:(n + 1) * PAIR, 0, :].bitcast(F32),
                             src[0:PAIR, 0, 0].rearrange("p a q -> p (a q)")).then_inc(q_first_loaded, 16)
            for which, src in enumerate((q_pair_hi, q_pair_lo)):
                sp.dma_start(q_dram[which, 0].rearrange("h r c -> r h c"),
                             src[:, :, 0].rearrange("p h a q -> p h (a q)")).then_inc(q0_stored, 16)
            ring.wait_taken(sp, [FUSE["K", n] for n in range(NCH)])
            stack_keys(0, range(0, 1))
            sp.wait_ge(q0_stored, 32)
            load_q(0, 0, range(1, 4), stacked[1])
            stack_keys(0, range(1, 4))
            sp.wait_ge(q_hi_stored, 32)
            sp.wait_ge(q_lo_ready, 3)
            sp.wait_ge(q_first_loaded, 48)
            load_context(sp, 1)
            ring.wait_taken(sp, [FUSE["K", NCH + n] for n in range(NCH)])
            load_q(0, 1)
            stack_keys(1)
            sp.wait_ge(q_lo_stored, 32)

            def body(b, more):
                def known(v):
                    return v if type(v) is int else sp.snap(v)

                in_loop = type(b) is not int
                mask_at = known((b + 1) * (LQ * LK) if in_loop else b + 1)
                q_at = known((b + 1) * (DH * P * P) if in_loop else b + 1)
                context_at = known((b + 2) * (LK * D) if in_loop else b + 2)
                made = known(b + 1)
                half_scored, scored = known(b * G + G // 2), known(b * G + G)
                turns = known(b * ring.turns)
                transposed = known(turns + (use(("C", NC - 1)) // 3 + 1))
                projected = [[(n, known(turns + c)) for n, c in ring.last_fills([use(("K", half * NCH + n)) for n in range(NCH)])]
                             for half in range(DH)]
                sp.wait_ge(mask_ready, made)
                sp.nop(nofuse=True)
                load_mask(mask_at)
                sp.wait_ge(scores_ready, half_scored)
                sp.nop(nofuse=True)
                load_q(q_at, 0)
                if more:
                    sp.wait_ge(ring.filled[use(("C", NC - 1)) % 3], transposed)
                    sp.nop(nofuse=True)
                    load_context(sp, context_at)
                for n, count in projected[0]:
                    sp.wait_ge(ring.freed[n], count)
                    sp.nop(nofuse=True)
                stack_keys(0)
                sp.wait_ge(scores_ready, scored)
                sp.nop(nofuse=True)
                load_q(q_at, 1)
                for n, count in projected[1]:
                    sp.wait_ge(ring.freed[n], count)
                    sp.nop(nofuse=True)
                stack_keys(1)

            with sp.Fori(0, LAST - 1) as b:
                body(b, True)
            body(LAST - 1, False)
            for g in range(G):
                sp.wait_ge(stacked[g], stackings(g, LAST))
            for n, w in enumerate((sWq, sWk, sWv, sWo, fWr, fWk, fWv)):
                w = w.rearrange("h d e -> (h d) e") if len(w.shape) == 3 else w
                sp.dma_start(w_nat[:, n], w.rearrange("(t p) n -> p t n", p=P)).then_inc(tail_w_loaded, 16)
            out_t = out.rearrange("(j b) q d -> (b q) j d", b=2)
            for j in range(TJ):
                sp.wait_ge(sum_ready, j + 1)
                sp.dma_start(out_t[:, j, :], xres[:, j, :]).then_inc(out_stored, 16)
            sp.wait_ge(out_stored, 16 * TJ)

        @block.gpsimd
        def _(pool):
            for n, v in enumerate((bq, bk)):
                pool.dma_start(cols[:, n, :], v.rearrange("(t p) -> p t", p=P),
                               allow_slow_non_contiguous=True).then_inc(bias_loaded, 16)
            pool.memset(ctxT_hi[:, :, LK:KPAD].bitcast(F32), 0.0).then_inc(pads_ready, 1)
            pool.memset(ctxT_lo[:, :, LK:KPAD].bitcast(F32), 0.0).then_inc(pads_ready, 1)
            pool.memset(mask_add[:, LK:KS], PADDED).then_inc(pads_ready, 1)
            for n in range(2):
                pool.dma_start(bv_row[:, n, :], bv.rearrange("(a n) -> a n", a=1).broadcast_to([P, D]))\
                    .then_inc(small_loaded, 16)
            pool.dma_start(bo_row[:, :], bo.rearrange("(a n) -> a n", a=1).broadcast_to([P, D])).then_inc(small_loaded, 16)
            pool.dma_start(wo[:, :, :], Wo.rearrange("(t p) n -> p t n", p=P)).then_inc(small_loaded, 16)
            for n, v in enumerate((sbq, sbk, sbv)):
                pool.dma_start(sbv_col[:, n, :], v.rearrange("h d -> (h d)").rearrange("(t p) -> p t", p=P),
                               allow_slow_non_contiguous=True)\
                    .then_inc(small_loaded, 16)
            pool.dma_start(sbo_row[:, :], sbo.rearrange("(a n) -> a n", a=1).broadcast_to([P, D]))\
                .then_inc(small_loaded, 16)
            for n, v in enumerate((mu_r, mu_k)):
                pool.dma_start(mus[:, n, 0, :], v.rearrange("(t p) -> p t", p=P),
                               allow_slow_non_contiguous=True).then_inc(small_loaded, 16)
            pool.wait_ge(w_hi_ready, 2)
            nc.gpsimd.tensor_tensor(wv_lo[:, :, :], w_raw[:, 2], wv_hi[:, :, :], ALU.subtract).then_inc(wv_ready, 1)
            for which, (src, ready, count) in enumerate(((q_pair_hi, q_hi_ready, 2), (q_pair_lo, q_lo_ready, 3))):
                pool.wait_ge(ready, count)
                for half in range(DH):
                    pool.dma_start(q_dram[which, 1:B, half].rearrange("b r c -> r b c"),
                                   src[:, half, 1:B].rearrange("p b a q -> p b (a q)")).then_inc((q_hi_stored, q_lo_stored)[which], 16)
            pool.wait_ge(small_loaded, SMALL)
            pool.wait_ge(xn_ready, TJ)
            for j in range(TJ):
                nc.gpsimd.tensor_tensor(xres[:, j, :], xres[:, j, :], bo_row[:, :], ALU.add).then_inc(bo_added, 1)

            def add_bias(j):
                pool.wait_ge(xn2_ready, j + 1)
                nc.gpsimd.tensor_tensor(xres[:, j, :], xres[:, j, :], sbo_row[:, :], ALU.add).then_inc(bias_added, 1)

            for j in range(EARLY):
                add_bias(j)
            pool.wait_ge(pv_free, 2 * B + 1)
            for j in range(TJ):
                wait_qk(pool, j)
                if j >= 2:
                    tring.wait_filled(pool, TUSE["S1", j - 2])
                for b2 in range(2):
                    nc.gpsimd.tensor_tensor(
                        k2_diag[:, (j % 2) * 4 + 2 + b2],
                        k2T[:, j, 1, b2 * LQ:(b2 + 1) * LQ].unsqueeze(1).broadcast_to([P, HH, LQ]),
                        head_mask.unsqueeze(2).broadcast_to([P, HH, LQ]), ALU.mult).then_inc(diag_ready[1], 1)
                if j == 1:
                    add_bias(TJ - 1)


        @block.scalar
        def _(act):
            def copy(dst, src):
                return nc.scalar.activation(dst, src, ACT.Copy)

            def context_hi(n, u, b):
                tiles = min(2, KT - 2 * n)
                width = P * tiles if n < NC - 1 else KTAIL
                ring.wait_filled(act, u, b)
                src = ring.bank(u)[:, :].rearrange("p (t k) -> p t k", t=DH)[:, :, 0:width]
                copy(ctxT_hi[:, :, 2 * n * P:2 * n * P + width], src).then_inc(hi_ready, 1)

            def keys_hi(n, u, b, first=False):
                half, c = divmod(n, NCH)
                ring.wait_filled(act, u, b)
                if c == 0 and not first:
                    for g in range(4 * half, 4 * half + 4):
                        act.wait_ge(stacked[g], stackings(g, b))
                nc.scalar.activation(keysT[:, 0, half, c * CH:(c + 1) * CH].bitcast(F32R), ring.bank(u)[:, 0:CH],
                                     ACT.Identity, bias=cols[:, 1, half:half + 1]).then_inc(hi_ready, 1)

            def exps(b, g):
                s = b * G + g
                act.wait_ge(masked_ready, s + 1)
                nc.scalar.activation(probs[:, g % 2, 0:KS], probs[:, g % 2, 0:KS], ACT.Exp,
                                     bias=xmin[:, g % 2:g % 2 + 1], scale=-1.0,
                                     accum_out=psums[:, g:g + 1]).then_inc(probs_ready, 1)

            def take_qk(j, bank, freed):
                for n, dst in enumerate((q2T, k2T)):
                    for half in range(DH):
                        at = (n * DH + half) * P
                        last = nc.scalar.activation(dst[:, j, half], bank[:, at:at + P], ACT.Identity,
                                                    bias=sbv_col[:, n, half:half + 1])
                last.then_inc(freed, 1)

            for n in range(NC):
                context_hi(n, FUSE["C", n], 0)
                if n == 2:
                    for half in range(DH):
                        xq.wait_filled(act, XQ["X", half])
                        copy(xnT[:, half, :], xq.bank(XQ["X", half])).then_inc(xq.freed[XQ["X", half]], 1)
                if n == 3:
                    for i, hi in ((1, wk_hi), (2, wv_hi)):
                        act.wait_ge(w_loaded[i], 16)
                        copy(hi[:, :, :], w_raw[:, i]).then_inc(w_hi_ready, 1)
                if n == NC - 1:
                    act.wait_ge(q_scale_ready, 1)
                    for half in range(DH):
                        xq.wait_filled(act, XQ["Q", half])
                        for h2 in range(2):
                            last = nc.scalar.activation(
                                q_pair[:, half, :, h2, :], xq.bank(XQ["Q", half]).rearrange("p (b q) -> p b q", q=LQ),
                                ACT.Identity, bias=q_bias[:, half, h2:h2 + 1], scale=q_scale[:, h2:h2 + 1])
                        last.then_inc(xq.freed[XQ["Q", half]], 1)
            xq.wait_taken(act, [XQ["Q", half] for half in range(DH)])
            def q_hi(lo, hi):
                copy(q_pair_hi[:, :, lo:hi].rearrange("p t b a q -> p t (b a q)").bitcast(F32R),
                     q_pair[:, :, lo:hi].rearrange("p t b a q -> p t (b a q)")).then_inc(q_hi_ready, 1)

            q_hi(0, 1)
            for n in range(NK):
                keys_hi(n, FUSE["K", n], 0, first=True)
            q_hi(1, B)
            exps(0, 0)

            def body(b, last):
                for g in range(G):
                    if g == Q_LO_TILE:
                        act.wait_ge(q_lo_stored, 32)
                    for kind, n in (WORK_LAST if last else WORK)[g]:
                        u = use(("P", g, n) if kind == "P" else (kind, n), last)
                        if kind == "P":
                            ring.wait_filled(act, u, b)
                            bank, tiles = ring.bank(u), PT_TILES[n]
                            done = copy(probsT[:, g % 4, tiles[0]:tiles[-1] + 1, :],
                                        bank[:, 0:len(tiles) * P].rearrange("p (t c) -> p t c", c=P))
                            if g % 4 == 3 and n == LAST_PT:
                                done = copy(recipT[:, :], bank[:, 3 * P:4 * P])
                            done.then_inc(ring.freed[u % 3], 1)
                        if kind == "P" and n == LAST_PT and g < G - 1:
                            exps(b, g + 1)
                        elif kind == "P" and n == LAST_PT and not last:
                            exps(b + 1, 0)
                        if kind == "C":
                            context_hi(n, u, b)
                        if kind == "W":
                            ring.wait_filled(act, u, b)
                            copy(wT(n)[:, :, :], ring.bank(u)[:, :].rearrange("p (t d) -> p t d", t=DH))\
                                .then_inc(ring.freed[u % 3], 1)
                        if kind == "K":
                            keys_hi(n, u, b)
                        if kind == "X":
                            ring.wait_filled(act, u, b)
                            nc.scalar.activation(xnT2[:, n].rearrange("p t c -> p (t c)"), ring.bank(u)[:, 0:D], ACT.Copy)\
                                .then_inc(ring.freed[u % 3], 1)

            with act.Fori(0, LAST) as b:
                body(b, False)
            body(LAST, True)

            act.wait_ge(pv_free, 2 * B + 1)
            for stage, j in TAIL:
                u = TUSE[stage, j]
                if stage in ("Y", "O", "Y2", "FV"):
                    continue
                tring.wait_filled(act, u)
                bank, freed = tring.bank(u), tring.freed[u % tring.n]
                if stage == "X":
                    copy(xnT2[:, j].rearrange("p t c -> p (t c)"), bank[:, 0:D]).then_inc(freed, 1)
                elif stage == "QK":
                    take_qk(j, bank, freed)
                elif stage == "V":
                    for h2 in range(2):
                        last = nc.scalar.activation(
                            v2[:, 2 * j:2 * j + 2, :, h2 * VW:h2 * VW + DK].rearrange("p b g d -> p (b g) d"),
                            bank[:, :].rearrange("p (a h d) -> p a h d", h=2, d=DK)[:, :, h2, :],
                            ACT.Identity, scale=pair_mask[:, h2 * DK:h2 * DK + 1])
                    last.then_inc(freed, 1)
                elif stage in ("S0", "S1"):
                    half = int(stage[1])
                    tring.wait_taken(act, [u])
                    rows = p2[:, (j % 2) * 2 + half]
                    nc.scalar.activation(rows, rows, ACT.Exp, scale=DK ** -0.5).then_inc(p2_ready[half], 1)
                elif stage in ("T0", "T1"):
                    if j >= 2:
                        tring.wait_filled(act, TUSE["O", j - 2])
                    copy(p2T[:, (j % 2) * 2 + int(stage[1])], bank[:, :].rearrange("p (g c) -> p g c", c=P))                        .then_inc(freed, 1)
                elif stage == "OT":
                    for half in range(DH):
                        last = nc.scalar.activation(attnT[:, half, j * P:(j + 1) * P], bank[:, half * P:(half + 1) * P],
                                                    ACT.Identity, bias=sbv_col[:, 2, half:half + 1])
                    last.then_inc(freed, 1)
                elif stage == "X3":
                    for n, dst in ((0, xrT), (1, xkT)):
                        for half in range(DH):
                            last = nc.scalar.activation(dst[:, j, half], bank[:, half * P:(half + 1) * P],
                                                        ACT.Copy, scale=mus[:, n, 0, half:half + 1])
                    last.then_inc(scaled_ready, 1)
                elif stage == "F":
                    keys = kaT[:, j].rearrange("p t c -> p (t c)")
                    nc.scalar.activation(keys, bank[:, 0:D], ACT.Relu).then_inc(relu_ready, 1)
                    nc.scalar.activation(gate[:, j], bank[:, D:2 * D], ACT.Tanh, scale=0.5).then_inc(freed, 1)
                    act.wait_ge(relu_ready, j + 1)
                    nc.scalar.activation(keys, keys, ACT.Square).then_inc(ka_ready, 1)

        @block.vector
        def _(dve):
            steps = [0]

            def link(ins):
                steps[0] += 1
                ins.then_inc(dve_step, 1)
                dve.wait_ge(dve_step, steps[0])

            def layernorm(tiles, dst, ready):
                j0, n = tiles[0], len(tiles)
                for j in tiles:
                    last = nc.vector.bn_stats(stats[:, j, :], xres[:, j, :])
                link(last)
                for j in tiles:
                    last = nc.vector.bn_aggr(mv[:, j, :], stats[:, j, :])
                link(last)
                v = [newton[:, i, 0:n] for i in range(3)]
                y, t, bits = newton[:, 3, 0:n], newton[:, 4, 0:n], newton_bits[:, 0, 0:n]
                link(nc.vector.tensor_scalar(v[0], mv[:, j0:j0 + n, 1], EPS, None, ALU.add))
                nc.vector.tensor_scalar(v[1], v[0], 0.25, None, ALU.mult)
                nc.vector.tensor_scalar(v[2], v[0], 0.0625, None, ALU.mult)
                link(nc.vector.tensor_scalar(bits, v[0].bitcast(I32), 1, None, ALU.logical_shift_right))
                link(nc.vector.tensor_scalar(y.bitcast(I32), bits, -1, RSQRT_SEED, ALU.mult, ALU.add))
                for i in range(3):
                    if n == 1:
                        link(nc.vector.scalar_tensor_tensor(out=t, in0=y, scalar=v[i], in1=y, op0=ALU.mult, op1=ALU.mult))
                    else:
                        link(nc.vector.tensor_tensor(t, y, y, ALU.mult))
                        link(nc.vector.tensor_tensor(t, t, v[i], ALU.mult))
                    link(nc.vector.scalar_tensor_tensor(out=y, in0=t, scalar=-3.0, in1=y, op0=ALU.add, op1=ALU.mult))
                link(nc.vector.tensor_scalar(rstd[:, j0:j0 + n], y, -0.125, None, ALU.mult))
                for j in tiles:
                    nc.vector.tensor_scalar(dst[:, j, :], xres[:, j, :], mv[:, j, 0:1], rstd[:, j:j + 1],
                                            ALU.subtract, ALU.mult).then_inc(ready, 1)

            def add_projection(j, bank, freed):
                nc.vector.tensor_tensor(xres[:, j, :], bank[:, 0:D], xres[:, j, :], ALU.add).then_inc(freed, 1)

            dve.wait_ge(x_loaded, 32)
            layernorm(range(TJ), xn, xn_ready)
            dve.wait_ge(bias_loaded, 32)
            nc.vector.tensor_scalar(q_scale[:, :], side_mask, QSCALE, None, ALU.mult)
            for half in range(DH):
                last = nc.vector.tensor_scalar(q_bias[:, half, :], side_mask, cols[:, 0, half:half + 1], QSCALE,
                                               ALU.mult, ALU.mult)
            last.then_inc(q_scale_ready, 1)

            def make_mask(b):
                dve.wait_ge(mask_loaded, (b + 1) * 32)
                nc.vector.tensor_scalar(mask_add[:, 0:LK], mask_b[:, :], MASKED, None, ALU.mult).then_inc(mask_ready, 1)
                dve.wait_ge(mask_ready, b + 1)

            def context_lo(n, u, b, at):
                tiles = min(2, KT - 2 * n)
                width = P * tiles if n < NC - 1 else KTAIL
                dve.wait_ge(hi_ready, at)
                src = ring.bank(u)[:, :].rearrange("p (t k) -> p t k", t=DH)[:, :, 0:width]
                nc.vector.tensor_tensor(ctxT_lo[:, :, 2 * n * P:2 * n * P + width], src,
                                        ctxT_hi[:, :, 2 * n * P:2 * n * P + width], ALU.subtract)\
                    .then_inc(ring.freed[u % 3], 1)

            def keys_lo(n, u, b, at):
                half, c = divmod(n, NCH)
                dve.wait_ge(hi_ready, at)
                nc.vector.scalar_tensor_tensor(
                    out=keysT[:, 1, half, c * CH:(c + 1) * CH].bitcast(F32R), in0=ring.bank(u)[:, 0:CH],
                    scalar=cols[:, 1, half:half + 1], in1=keysT[:, 0, half, c * CH:(c + 1) * CH],
                    op0=ALU.add, op1=ALU.subtract).then_inc(ring.freed[u % 3], 1)

            def mask_scores(b, g):
                dve.wait_ge(scores_ready, b * G + g + 1)
                dve.nop(nofuse=True)
                nc.vector.tensor_tensor_reduce(
                    out=probs[:, g % 2, 0:KS].rearrange("p (n c) -> p n c", n=NCH),
                    in0=score_banks[:, :, 0:CH], in1=mask_add[:, :].rearrange("p (n c) -> p n c", n=NCH),
                    scale=1.0, scalar=3.0e38, op0=ALU.add, op1=ALU.min,
                    accum_out=xmin[:, g % 2:g % 2 + 1]).then_inc(masked_ready, 1)

            HI = NC + NK
            def q_lo(step, half, lo, hi):
                dve.wait_ge(q_hi_ready, step)
                flat = [v[:, half, lo:hi].rearrange("p b a q -> p (b a q)") for v in (q_pair, q_pair_hi, q_pair_lo)]
                return nc.vector.tensor_tensor(flat[2].bitcast(F32R), flat[0], flat[1], ALU.subtract)

            for n in range(NC):
                context_lo(n, FUSE["C", n], 0, n + 1)
                if n == 3:
                    dve.wait_ge(w_hi_ready, 1)
                    nc.vector.tensor_tensor(wk_lo[:, :, :], w_raw[:, 1], wk_hi[:, :, :], ALU.subtract).then_inc(wk_ready, 1)
            q_lo(1, 0, 0, 1)
            q_lo(1, 1, 0, 1).then_inc(q_lo_ready, 1)
            nc.vector.memset(probs[:, :, KS:KPAD], 0.0).then_inc(pv_free, 1)
            for n in range(NK):
                keys_lo(n, FUSE["K", n], 0, NC + n + 1)
                if n == 2:
                    dve.wait_ge(pads_ready, PADS)
                    make_mask(0)
            dve.wait_ge(pv_free, 1)
            mask_scores(0, 0)
            for half in range(DH):
                q_lo(2, half, 1, B).then_inc(q_lo_ready, 1)
            dve.wait_ge(small_loaded, SMALL)
            nc.vector.tensor_scalar(mus[:, :, 1, :], mus[:, :, 0, :], -1.0, 1.0, ALU.mult, ALU.add)

            def body(b, last):
                made = 0
                for g in range(G):
                    if g < G - 1:
                        mask_scores(b, g + 1)
                    elif not last:
                        make_mask(b + 1)
                        mask_scores(b + 1, 0)
                    for kind, n in (WORK_LAST if last else WORK)[g]:
                        u = use(("P", g, n) if kind == "P" else (kind, n), last)
                        if kind == "V":
                            ring.wait_filled(dve, u, b)
                            tiles = min(2, KT - 2 * n)
                            nc.vector.tensor_tensor(
                                values[:, 2 * n:2 * n + tiles, :],
                                ring.bank(u)[:, 0:tiles * D].rearrange("p (t d) -> p t d", d=D),
                                bv_row[:, 0:tiles, :], ALU.add).then_inc(ring.freed[u % 3], 1)
                        elif kind in "CK":
                            made += 1
                            (context_lo if kind == "C" else keys_lo)(n, u, b, (b + 1) * HI + made)
                        elif kind == "QK":
                            ring.wait_filled(dve, u, b)
                            for i, dst in enumerate((q2T, k2T)):
                                for half in range(DH):
                                    at = (i * DH + half) * P
                                    done = nc.vector.tensor_scalar(dst[:, n, half], ring.bank(u)[:, at:at + P],
                                                                   sbv_col[:, i, half:half + 1], None, ALU.add)
                            done.then_inc(ring.freed[u % 3], 1)
                        elif kind == "Y":
                            if n == 0:
                                dve.wait_ge(bo_added, TJ)
                                dve.wait_ge(tail_w_loaded, 16 * NW)
                            ring.wait_filled(dve, u, b)
                            add_projection(n, ring.bank(u), ring.freed[u % 3])
                            if n == EARLY - 1:
                                ring.wait_taken(dve, [use(("Y", j), last) for j in range(EARLY)], b)
                                layernorm(range(EARLY), xn2, xn2_ready)
                    if g % 4 == 2:
                        h = 2 * b + g // 4
                        dve.wait_ge(probs_ready, b * G + g + 2)
                        nc.vector.reciprocal(precip[:, :], psums[:, g - 2:g + 2]).then_inc(recip_step, 1)
                        dve.wait_ge(recip_step, h + 1)
                        nc.vector.tensor_tensor(
                            pair_recip[:, :, :], precip[:, :].unsqueeze(2).broadcast_to([P, 4, PAIR]),
                            pair_mask.unsqueeze(1).broadcast_to([P, 4, PAIR]), ALU.mult).then_inc(pair_recip_ready, 1)
                    if g % 4 == 3:
                        h = 2 * b + g // 4
                        dve.wait_ge(pv_ready, h + 1)
                        nc.vector.tensor_tensor(prod[:, :, :].rearrange("p h q -> p (h q)"), pv_bank[:, 0:P],
                                                recipT[:, :], ALU.mult).then_inc(prod_ready, 1)
                        dve.wait_ge(prod_ready, h + 1)
                        at = b * LQ
                        dst = attnT[:, g // 4, at:at + LQ] if type(b) is int else attnT[:, g // 4, bass.ds(at, LQ)]
                        nc.vector.tensor_tensor(dst, prod[:, 0, :], prod[:, 1, :], ALU.add).then_inc(pv_free, 1)

            with dve.Fori(0, LAST) as b:
                body(b, False)
            body(LAST, True)

            ones = v2.rearrange("p b g (h d) -> p (b g) h d", h=2)[:, :, :, DK]
            nc.vector.tensor_copy(ones, pair_mask.rearrange("p (h d) -> p h d", h=2)[:, :, 0].unsqueeze(1)
                                  .broadcast_to([P, TJ * 2 * G, 2])).then_inc(ones_ready, 1)
            for stage, j in TAIL:
                if stage in ("X", "QK", "T0", "T1", "OT", "F"):
                    continue
                u = TUSE[stage, j]
                if stage != "V":
                    tring.wait_filled(dve, u)
                bank, freed = tring.bank(u), tring.freed[u % tring.n]
                if stage == "Y":
                    add_projection(j, bank, freed)
                    tring.wait_taken(dve, [u])
                    layernorm([j], xn2, xn2_ready)
                elif stage == "V":
                    wait_qk(dve, j)
                    if j >= 2:
                        tring.wait_filled(dve, TUSE["S0", j - 2])
                    for b2 in range(2):
                        nc.vector.tensor_tensor(
                            k2_diag[:, (j % 2) * 4 + b2],
                            k2T[:, j, 0, b2 * LQ:(b2 + 1) * LQ].unsqueeze(1).broadcast_to([P, HH, LQ]),
                            head_mask.unsqueeze(2).broadcast_to([P, HH, LQ]), ALU.mult).then_inc(diag_ready[0], 1)
                elif stage in ("S0", "S1"):
                    half = int(stage[1])
                    s = bank[:, :].rearrange("p (h k) -> p h k", k=LQ)
                    link(nc.vector.tensor_reduce(max2[:, j, half, :], s, AX.X, ALU.max))
                    if j >= 2:
                        tring.wait_filled(dve, TUSE["T0" if half == 0 else "T1", j - 2])
                    nc.vector.tensor_tensor(p2[:, (j % 2) * 2 + half], s,
                                            max2[:, j, half, :].unsqueeze(2).broadcast_to([P, HH, LQ]),
                                            ALU.subtract).then_inc(freed, 1)
                elif stage == "O":
                    o = bank[:, 0:G * 2 * VW].rearrange("p (h d) -> p h d", d=VW)
                    link(nc.vector.reciprocal(recip2[:, j, :], o[:, :, DK]))
                    nc.vector.tensor_tensor(o2[:, j].rearrange("p (h d) -> p h d", d=DK), o[:, :, 0:DK],
                                            recip2[:, j, :].unsqueeze(2).broadcast_to([P, H, DK]), ALU.mult).then_inc(freed, 1)
                elif stage == "Y2":
                    dve.wait_ge(bias_added, j + 1)
                    add_projection(j, bank, freed)
                    tiles = next(t for t in NORM_TILES if j in t)
                    if j == tiles[-1]:
                        tring.wait_taken(dve, [TUSE["Y2", i] for i in tiles])
                        layernorm(tiles, xn2, xn3_ready)
                elif stage == "X3":
                    dve.wait_ge(scaled_ready, j + 1)
                    for n, dst in ((0, xrT), (1, xkT)):
                        for half in range(DH):
                            mixed = dst[:, j, half].rearrange("p (b q) -> p b q", q=LQ)[:, :, 1:LQ]
                            before = bank[:, half * P:(half + 1) * P].rearrange("p (b q) -> p b q", q=LQ)[:, :, 0:LQ - 1]
                            last = nc.vector.scalar_tensor_tensor(
                                out=mixed, in0=before, scalar=mus[:, n, 1, half:half + 1], in1=mixed,
                                op0=ALU.mult, op1=ALU.add)
                    last.then_inc(freed, 1)
                elif stage == "FV":
                    tring.wait_taken(dve, [TUSE["F", j]])
                    nc.vector.scalar_tensor_tensor(out=gate[:, j], in0=gate[:, j], scalar=1.0, in1=bank[:, 0:D],
                                                   op0=ALU.add, op1=ALU.mult).then_inc(freed, 1)
                    tring.wait_taken(dve, [u])
                    nc.vector.scalar_tensor_tensor(out=xres[:, j, :], in0=gate[:, j], scalar=0.5, in1=xres[:, j, :],
                                                   op0=ALU.mult, op1=ALU.add).then_inc(sum_ready, 1)

        @block.tensor
        def _(pe):
            def transposes(dst, srcs):
                for n, src in enumerate(srcs):
                    rows, width = src.shape[0], src.shape[1]
                    last = nc.tensor.transpose(dst[0:width, n * P:n * P + rows], src, ident[0:rows, 0:rows])
                return last

            def accumulate(dst, terms):
                for n, (a, c) in enumerate(terms):
                    last = nc.tensor.matmul(dst, a, c, start=(n == 0), stop=(n == len(terms) - 1))
                return last

            def three_passes(dst, terms):
                terms = [t for ah, al, bh, bl in terms for t in ((ah, bh), (al, bh), (ah, bl))]
                for n, (a, c) in enumerate(terms):
                    last = nc.tensor.matmul(dst, a, c, start=(n == 0), stop=(n == len(terms) - 1))
                return last

            def context_transposes(n, u, b, wait):
                ring.wait_free(pe, u, b)
                if wait is None:
                    for i, tiles in enumerate(PIECES):
                        if 2 * n in tiles or min(2 * n + 1, KT - 1) in tiles:
                            pe.wait_ge(piece_loaded[i], 16)
                elif n == 0:
                    pe.wait_ge(context_loaded, wait)
                bank = ring.bank(u)
                for half in range(DH):
                    for t in range(2 * n, min(2 * n + 2, KT)):
                        rows = P if t < KT - 1 else KTAIL
                        at = half * 2 * P + (t - 2 * n) * P
                        last = nc.tensor.transpose(bank[:, at:at + rows],
                                                   context[0:rows, t, half * P:(half + 1) * P], ident[0:rows, 0:rows])
                last.then_inc(ring.filled[u % 3], 1)

            def project_keys(n, u, b):
                half, c = divmod(n, NCH)
                ring.wait_free(pe, u, b)
                cs = slice(half * P, (half + 1) * P)
                ks = slice(c * CH, (c + 1) * CH)
                three_passes(ring.bank(u)[:, 0:CH],
                             [(wk_hi[:, t, cs], wk_lo[:, t, cs], ctxT_hi[:, t, ks], ctxT_lo[:, t, ks])
                              for t in range(DH)]).then_inc(ring.filled[u % 3], 1)

            def project_values(n, u, b):
                ring.wait_free(pe, u, b)
                for i, t in enumerate(range(2 * n, min(2 * n + 2, KT))):
                    ks = slice(t * P, (t + 1) * P)
                    last = three_passes(ring.bank(u)[:, i * D:(i + 1) * D],
                                        [(ctxT_hi[:, d, ks], ctxT_lo[:, d, ks], wv_hi[:, d, :], wv_lo[:, d, :])
                                         for d in range(DH)])
                last.then_inc(ring.filled[u % 3], 1)

            def project_output(j, bank, w):
                return accumulate(bank[:, 0:D], [(attnT[:, t, j * P:(j + 1) * P], w[:, t, :]) for t in range(DH)])

            def transpose_tokens(j, bank):
                return transposes(bank, [xn2[:, j, half * P:(half + 1) * P] for half in range(DH)])

            def project_qk(j, bank):
                for n, w in enumerate((W_Q, W_K)):
                    for half in range(DH):
                        at = (n * DH + half) * P
                        last = accumulate(bank[:, at:at + P], [(wT(w)[:, t, half * P:(half + 1) * P], xnT2[:, j, t])
                                                               for t in range(DH)])
                return last

            def scores(b, g):
                if type(b) is not int or b * G + g > 0:
                    pe.wait_ge(masked_ready, b * G + g)
                if g % 4 == 0:
                    pe.wait_ge(q_second_loaded if g else q_first_loaded, (b + 1) * 48)
                pe.wait_ge(stacked[g], stackings(g, b))
                for c in range(NCH):
                    last = nc.tensor.matmul(score_banks[:, c, 0:CH], q_stack[:, g, :],
                                            k_stack[:, g, c * CH:(c + 1) * CH], start=True, stop=True)
                last.then_inc(scores_ready, 1)

            for n in range(NC):
                if n == 3:
                    for half in range(DH):
                        pe.wait_ge(xn_ready, TJ)
                        transposes(xq.bank(XQ["X", half]), [xn[:, j, half * P:(half + 1) * P] for j in range(TJ)])\
                            .then_inc(xq.filled[XQ["X", half]], 1)
                context_transposes(n, FUSE["C", n], 0, None)
                if n == NC - 1:
                    xq.wait_taken(pe, [XQ["X", half] for half in range(DH)])
                    pe.wait_ge(w_loaded[0], 16)
                    for half in range(DH):
                        accumulate(xq.bank(XQ["Q", half]), [(w_raw[:, 0, t, half * P:(half + 1) * P], xnT[:, t, :])
                                                            for t in range(DH)]).then_inc(xq.filled[XQ["Q", half]], 1)
            pe.wait_ge(wk_ready, 1)
            pe.wait_ge(pads_ready, PADS)
            ring.wait_taken(pe, [FUSE["C", n] for n in range(NC)])
            for n in range(NK):
                project_keys(n, FUSE["K", n], 0)
            xq.wait_taken(pe, [XQ["Q", half] for half in range(DH)])
            scores(0, 0)
            pe.wait_ge(wv_ready, 1)

            def body(b, last_batch):
                for g in range(G):
                    if g < G - 1:
                        scores(b, g + 1)
                    elif not last_batch:
                        scores(b + 1, 0)
                    for kind, n in (WORK_LAST if last_batch else WORK)[g]:
                        u = use(("P", g, n) if kind == "P" else (kind, n), last_batch)
                        if kind == "P":
                            if n == 0:
                                pe.wait_ge(probs_ready, b * G + g + 1)
                            ring.wait_free(pe, u, b)
                            srcs = [probs[:, g % 2, t * P:(t + 1) * P] for t in PT_TILES[n]]
                            if g % 4 == 3 and n == LAST_PT:
                                pe.wait_ge(pair_recip_ready, 2 * b + g // 4 + 1)
                                srcs.append(pair_recip[:, :, :].rearrange("p a b -> p (a b)"))
                            transposes(ring.bank(u), srcs).then_inc(ring.filled[u % 3], 1)
                            continue
                        if kind == "V":
                            project_values(n, u, b)
                        elif kind == "C":
                            context_transposes(n, u, b, (b + 1) * 32)
                        elif kind == "W":
                            ring.wait_free(pe, u, b)
                            if n == 0:
                                pe.wait_ge(tail_w_loaded, 16 * NW)
                            for half in range(DH):
                                for t in range(DH):
                                    at = half * D + t * P
                                    last = nc.tensor.transpose(ring.bank(u)[:, at:at + P],
                                                               w_nat[:, n, t, half * P:(half + 1) * P], ident)
                            last.then_inc(ring.filled[u % 3], 1)
                        elif kind == "Y":
                            ring.wait_free(pe, u, b)
                            project_output(n, ring.bank(u), wo).then_inc(ring.filled[u % 3], 1)
                        elif kind == "X":
                            ring.wait_free(pe, u, b)
                            pe.wait_ge(xn2_ready, n + 1)
                            transpose_tokens(n, ring.bank(u)).then_inc(ring.filled[u % 3], 1)
                        elif kind == "QK":
                            ring.wait_taken(pe, [use((k, m), True) for k, m in (("X", n), ("W", NW - 1))], b)
                            ring.wait_free(pe, u, b)
                            project_qk(n, ring.bank(u)).then_inc(ring.filled[u % 3], 1)
                        else:
                            if n == 0:
                                ring.wait_taken(pe, [use(("C", m)) for m in range(NC)], b)
                            project_keys(n, u, b)
                    if g % 4 == 3:
                        need = [use(("P", i, f), last_batch) for i in range(g - 3, g + 1) for f in range(len(PT_TILES))]
                        if g == 3:
                            need = [use(("V", n), last_batch) for n in range(NV)] + need
                        pe.wait_ge(pv_free, 2 * b + g // 4 + 1)
                        ring.wait_taken(pe, need, b)
                        for t in range(KT):
                            for p in range(4):
                                ch = (g - 3 + p) * PAIR
                                last = nc.tensor.matmul(pv_bank[p * PAIR:(p + 1) * PAIR, 0:P],
                                                        values[:, t, ch:ch + PAIR], probsT[:, p, t, :],
                                                        start=(t == 0), stop=(t == KT - 1))
                        last.then_inc(pv_ready, 1)

            with pe.Fori(0, LAST) as b:
                body(b, False)
            body(LAST, True)

            ring.wait_taken(pe, [use(("P", G - 1, f), True) for f in range(len(PT_TILES))] + [use(("QK", EARLY - 1), True)], LAST)
            pe.wait_ge(masked_ready, B * G)
            pe.wait_ge(pv_free, 2 * B + 1)
            for stage, j in TAIL:
                u = TUSE[stage, j]
                tring.wait_free(pe, u)
                bank = tring.bank(u)
                if stage == "Y":
                    last = project_output(j, bank, wo)
                elif stage == "X":
                    pe.wait_ge(xn2_ready, j + 1)
                    last = transpose_tokens(j, bank)
                elif stage == "QK":
                    tring.wait_taken(pe, [TUSE["X", j]])
                    last = project_qk(j, bank)
                elif stage == "V":
                    for b2 in range(2):
                        for t in range(DH):
                            for h2 in range(2):
                                last = nc.tensor.matmul(bank[h2 * LQ:(h2 + 1) * LQ, b2 * D:(b2 + 1) * D],
                                                        xnT2[:, j, t, b2 * LQ:(b2 + 1) * LQ], wT(W_V)[:, t, :],
                                                        start=(t == 0), stop=(t == DH - 1), skip_group_check=True)
                elif stage in ("S0", "S1"):
                    half = int(stage[1])
                    wait_qk(pe, j)
                    pe.wait_ge(diag_ready[half], 2 * j + 2)
                    for b2 in range(2):
                        last = nc.tensor.matmul(bank[b2 * LQ:(b2 + 1) * LQ, :], q2T[:, j, half, b2 * LQ:(b2 + 1) * LQ],
                                                k2_diag[:, (j % 2) * 4 + half * 2 + b2].rearrange("p h k -> p (h k)"),
                                                start=True, stop=True)
                elif stage in ("T0", "T1"):
                    half = int(stage[1])
                    pe.wait_ge(p2_ready[half], j + 1)
                    flat = p2[:, (j % 2) * 2 + half].rearrange("p h k -> p (h k)")
                    last = transposes(bank, [flat[:, i * P:(i + 1) * P] for i in range(4)])
                elif stage == "O":
                    tring.wait_taken(pe, [TUSE[s, j] for s in ("V", "T0", "T1")])
                    if j == 0:
                        pe.wait_ge(ones_ready, 1)
                    for g in range(G):
                        for b2 in range(2):
                            last = nc.tensor.matmul(bank[b2 * LQ:(b2 + 1) * LQ, g * 2 * VW:(g + 1) * 2 * VW],
                                                    p2T[:, (j % 2) * 2 + g // 4, g % 4, b2 * LQ:(b2 + 1) * LQ],
                                                    v2[:, 2 * j + b2, g, :], start=True, stop=True, skip_group_check=True)
                elif stage == "OT":
                    tring.wait_taken(pe, [TUSE["O", j]])
                    last = transposes(bank, [o2[:, j, half * P:(half + 1) * P] for half in range(DH)])
                elif stage == "Y2":
                    tring.wait_taken(pe, [TUSE["OT", j]])
                    last = project_output(j, bank, wT(W_O))
                elif stage == "X3":
                    pe.wait_ge(xn3_ready, j + 1)
                    last = transpose_tokens(j, bank)
                elif stage == "F":
                    tring.wait_taken(pe, [TUSE["X3", j]])
                    for half in range(DH):
                        accumulate(bank[:, half * P:(half + 1) * P],
                                   [(wT(W_FK)[:, t, half * P:(half + 1) * P], xkT[:, j, t]) for t in range(DH)])
                    last = accumulate(bank[:, D:2 * D], [(xrT[:, j, t], wT(W_FR)[:, t, :]) for t in range(DH)])
                else:
                    pe.wait_ge(ka_ready, j + 1)
                    last = accumulate(bank[:, 0:D], [(kaT[:, j, t], wT(W_FV)[:, t, :]) for t in range(DH)])
                last.then_inc(tring.filled[u % tring.n], 1)


_INS = ["x", "ctx_1024", "mask_BxSxS2_bf0",
        "L0_xattn_Wq", "L0_xattn_bq", "L0_xattn_Wk", "L0_xattn_bk", "L0_xattn_Wv", "L0_xattn_bv",
        "L0_xattn_Wo", "L0_xattn_bo",
        "L0_attn_Wq", "L0_attn_bq", "L0_attn_Wk", "L0_attn_bk", "L0_attn_Wv", "L0_attn_bv",
        "L0_attn_Wo", "L0_attn_bo",
        "L0_ffn_W_r", "L0_ffn_W_k", "L0_ffn_W_v", "L0_ffn_mu_r", "L0_ffn_mu_k"]


def shape_constants(np):
    c = np.zeros((P, CONSTS), np.float32)
    row = np.arange(P)
    c[:, C_ID:C_ID + P] = np.eye(P, dtype=np.float32)
    c[:, C_PAIR:C_PAIR + 32] = (row[:, None] // 64) == (np.arange(32)[None, :] // 16)
    c[:, C_HEAD:C_HEAD + 8] = (row[:, None] // 16) == np.arange(8)[None, :]
    c[:, C_SIDE:C_SIDE + 2] = (row[:, None] // 16) % 2 == np.arange(2)[None, :]
    return c


def kernel(**inputs):
    import numpy as _np
    import concourse.bacc as _bacc
    from concourse import mybir as _mybir
    from concourse.bass_utils import run_bass_kernel_spmd as _run

    nc = _bacc.Bacc("TRN2", target_bir_lowering=False, num_devices=1)
    arrays, args = {}, []
    for name in _INS:
        a = _np.ascontiguousarray(inputs[name])
        arrays[f"in_{name}_dram"] = a
        args.append(nc.dram_tensor(f"in_{name}_dram", a.shape, _mybir.dt.from_np(a.dtype), kind="ExternalInput").ap())
    a = shape_constants(_np)
    arrays["in_consts_dram"] = a
    args.append(nc.dram_tensor("in_consts_dram", a.shape, _mybir.dt.from_np(a.dtype), kind="ExternalInput").ap())
    args.append(nc.dram_tensor("out_0_dram", (8, 64, 256), _mybir.dt.float32, kind="ExternalOutput").ap())
    perceiver_layer(nc, *args)
    r = _run(nc, [arrays], core_ids=[0])
    return r.results[0]["out_0_dram"]
```
